# Optimizing a Trainium2 kernel written in Bass

```python
import numpy as np
import jax
import jax.numpy as jnp

def _softmax(x, axis=-1):
    return jax.nn.softmax(x, axis=axis)
def _gelu(x):
    return jax.nn.gelu(x, approximate=True)
def _silu(x):
    return jax.nn.silu(x)
def _sigmoid(x):
    return jax.nn.sigmoid(x)
def _layernorm(x, axis=-1, eps=1e-5):
    m = jnp.mean(x, axis=axis, keepdims=True)
    v = jnp.var(x, axis=axis, keepdims=True)
    return (x - m) / jnp.sqrt(v + eps)
def _scatter_add(tgt, idx, src, axis=0):
    return tgt.at[idx].add(src)
def _segment_sum(src, seg, n):
    return jax.ops.segment_sum(src, seg, n)

kernel_name = 'mk_conv_preact_d1_conv_nhwc384_676baf'

def setup_inputs(seed: int = 0):
    np.random.seed(seed)
    _w = jnp.asarray
    def _rec_inputs():
        import jax
        import jax.numpy as jnp
        _gk = jax.random.key(seed)
        x = -0.0004039 + 1 * jax.random.normal(jax.random.fold_in(_gk, 1), (8, 64, 64, 384), jnp.float32)
        return x
    x = _rec_inputs()
    def _L0_conv_setup():
        import jax, jax.numpy as jnp
        import numpy as np
        D_MODEL = 384
        D_STATE = 16
        D_CONV = 3
        EXPAND = 2
        D_INNER = EXPAND * D_MODEL
        HEADDIM = 64
        NHEADS = D_INNER // HEADDIM
        NGROUPS = 1
        CHUNK = 64
        D_IN_PROJ = 2 * D_INNER + 2 * NGROUPS * D_STATE + NHEADS
        CONV_DIM = D_INNER + 2 * NGROUPS * D_STATE

        def segsum(x):
            T = x.shape[-1]
            xe = jnp.broadcast_to(x[..., None], x.shape + (T,))
            mask_strict = jnp.tril(jnp.ones((T, T), bool), -1)
            xe = jnp.where(mask_strict, xe, 0.0)
            x_segsum = jnp.cumsum(xe, axis=-2)
            mask_incl = jnp.tril(jnp.ones((T, T), bool), 0)
            return jnp.where(mask_incl, x_segsum, -jnp.inf)

        def ssd_minimal_discrete(X, A, Bm, Cm, block_len):
            b, seqlen, h, p = X.shape
            c = seqlen // block_len
            X = X.reshape(b, c, block_len, h, p)
            Bm = Bm.reshape(b, c, block_len, h, -1)
            Cm = Cm.reshape(b, c, block_len, h, -1)
            A = A.reshape(b, c, block_len, h).transpose(0, 3, 1, 2)
            A_cumsum = jnp.cumsum(A, axis=-1)
            L = jnp.exp(segsum(A))
            Y_diag = jnp.einsum('bclhn,bcshn,bhcls,bcshp->bclhp', Cm, Bm, L, X)
            decay_states = jnp.exp(A_cumsum[:, :, :, -1:] - A_cumsum)
            states = jnp.einsum('bclhn,bhcl,bclhp->bchpn', Bm, decay_states, X)
            init = jnp.zeros_like(states[:, :1])
            states = jnp.concatenate([init, states], axis=1)
            A_last = jnp.pad(A_cumsum[:, :, :, -1], ((0, 0), (0, 0), (1, 0)))
            decay_chunk = jnp.exp(segsum(A_last))
            new_states = jnp.einsum('bhzc,bchpn->bzhpn', decay_chunk, states)
            states, final_state = (new_states[:, :-1], new_states[:, -1])
            state_decay_out = jnp.exp(A_cumsum)
            Y_off = jnp.einsum('bclhn,bchpn,bhcl->bclhp', Cm, states, state_decay_out)
            Y = (Y_diag + Y_off).reshape(b, seqlen, h, p)
            return (Y, final_state)
        key = jax.random.key(seed)
        ks = jax.random.split(key, 10)
        x = jax.random.normal(ks[0], (8, 64, 64, D_MODEL), jnp.float32)
        W_in = jax.random.normal(ks[1], (D_MODEL, D_IN_PROJ), jnp.float32) * 0.02
        W_conv = jax.random.normal(ks[2], (D_CONV, D_CONV, 1, CONV_DIM), jnp.float32) * 0.1
        b_conv = jax.random.normal(ks[3], (CONV_DIM,), jnp.float32) * 0.01
        dt = jnp.exp(jax.random.uniform(ks[4], (NHEADS,)) * (np.log(0.1) - np.log(0.001)) + np.log(0.001))
        dt = jnp.clip(dt, 0.0001, None)
        dt_bias = dt + jnp.log(-jnp.expm1(-dt))
        A_log = jnp.log(jax.random.uniform(ks[5], (NHEADS,), minval=1.0, maxval=16.0))
        D_param = jnp.ones((NHEADS,), jnp.float32)
        gamma = jnp.ones((D_INNER,), jnp.float32)
        beta = jnp.zeros((D_INNER,), jnp.float32)
        W_out = jax.random.normal(ks[6], (D_INNER, D_MODEL), jnp.float32) * 0.02
        return {'x': x, 'W_in': W_in, 'W_conv': W_conv, 'b_conv': b_conv, 'dt_bias': dt_bias, 'A_log': A_log, 'D_param': D_param, 'gamma': gamma, 'beta': beta, 'W_out': W_out}
    _L0_conv_all = _L0_conv_setup()
    _L0_conv_in = {k: v for k, v in _L0_conv_all.items() if k in ('W_in', 'W_conv', 'b_conv', 'dt_bias', 'A_log', 'D_param', 'gamma', 'beta', 'W_out', )}
    del _L0_conv_all

    return {
        "x": x,
        "L0_conv_W_in": _L0_conv_in["W_in"],
        "L0_conv_W_conv": _L0_conv_in["W_conv"],
        "L0_conv_b_conv": _L0_conv_in["b_conv"],
        "L0_conv_dt_bias": _L0_conv_in["dt_bias"],
        "L0_conv_A_log": _L0_conv_in["A_log"],
        "L0_conv_D_param": _L0_conv_in["D_param"],
        "L0_conv_gamma": _L0_conv_in["gamma"],
        "L0_conv_beta": _L0_conv_in["beta"],
        "L0_conv_W_out": _L0_conv_in["W_out"],
    }

def reference(x, L0_conv_W_in, L0_conv_W_conv, L0_conv_b_conv, L0_conv_dt_bias, L0_conv_A_log, L0_conv_D_param, L0_conv_gamma, L0_conv_beta, L0_conv_W_out):
    import jax
    import jax.numpy as jnp
    def _L0_conv_ref(x, W_in, W_conv, b_conv, dt_bias, A_log, D_param, gamma, beta, W_out):
        import jax, jax.numpy as jnp
        import numpy as np
        D_MODEL = 384
        D_STATE = 16
        D_CONV = 3
        EXPAND = 2
        D_INNER = EXPAND * D_MODEL
        HEADDIM = 64
        NHEADS = D_INNER // HEADDIM
        NGROUPS = 1
        CHUNK = 64
        D_IN_PROJ = 2 * D_INNER + 2 * NGROUPS * D_STATE + NHEADS
        CONV_DIM = D_INNER + 2 * NGROUPS * D_STATE

        def segsum(x):
            T = x.shape[-1]
            xe = jnp.broadcast_to(x[..., None], x.shape + (T,))
            mask_strict = jnp.tril(jnp.ones((T, T), bool), -1)
            xe = jnp.where(mask_strict, xe, 0.0)
            x_segsum = jnp.cumsum(xe, axis=-2)
            mask_incl = jnp.tril(jnp.ones((T, T), bool), 0)
            return jnp.where(mask_incl, x_segsum, -jnp.inf)

        def ssd_minimal_discrete(X, A, Bm, Cm, block_len):
            b, seqlen, h, p = X.shape
            c = seqlen // block_len
            X = X.reshape(b, c, block_len, h, p)
            Bm = Bm.reshape(b, c, block_len, h, -1)
            Cm = Cm.reshape(b, c, block_len, h, -1)
            A = A.reshape(b, c, block_len, h).transpose(0, 3, 1, 2)
            A_cumsum = jnp.cumsum(A, axis=-1)
            L = jnp.exp(segsum(A))
            Y_diag = jnp.einsum('bclhn,bcshn,bhcls,bcshp->bclhp', Cm, Bm, L, X)
            decay_states = jnp.exp(A_cumsum[:, :, :, -1:] - A_cumsum)
            states = jnp.einsum('bclhn,bhcl,bclhp->bchpn', Bm, decay_states, X)
            init = jnp.zeros_like(states[:, :1])
            states = jnp.concatenate([init, states], axis=1)
            A_last = jnp.pad(A_cumsum[:, :, :, -1], ((0, 0), (0, 0), (1, 0)))
            decay_chunk = jnp.exp(segsum(A_last))
            new_states = jnp.einsum('bhzc,bchpn->bzhpn', decay_chunk, states)
            states, final_state = (new_states[:, :-1], new_states[:, -1])
            state_decay_out = jnp.exp(A_cumsum)
            Y_off = jnp.einsum('bclhn,bchpn,bhcl->bclhp', Cm, states, state_decay_out)
            Y = (Y_diag + Y_off).reshape(b, seqlen, h, p)
            return (Y, final_state)
        Bsz, H, W, C = x.shape
        L = H * W
        xf = x.reshape(Bsz, L, C)
        zxbcdt = xf @ W_in
        z = zxbcdt[..., :D_INNER]
        xBC = zxbcdt[..., D_INNER:D_INNER + CONV_DIM]
        dt = jax.nn.softplus(zxbcdt[..., D_INNER + CONV_DIM:] + dt_bias)
        xBC = xBC.reshape(Bsz, H, W, CONV_DIM)
        xBC = jax.lax.conv_general_dilated(xBC, W_conv, window_strides=(1, 1), padding='SAME', dimension_numbers=('NHWC', 'HWIO', 'NHWC'), feature_group_count=CONV_DIM) + b_conv
        xBC = jax.nn.silu(xBC).reshape(Bsz, L, CONV_DIM)
        x_inner = xBC[..., :D_INNER].reshape(Bsz, L, NHEADS, HEADDIM)
        gn = NGROUPS * D_STATE
        B_state = xBC[..., D_INNER:D_INNER + gn].reshape(Bsz, L, NGROUPS, D_STATE)
        C_state = xBC[..., D_INNER + gn:].reshape(Bsz, L, NGROUPS, D_STATE)
        rep = NHEADS // NGROUPS
        B_state = jnp.broadcast_to(B_state[:, :, :, None, :], (Bsz, L, NGROUPS, rep, D_STATE)).reshape(Bsz, L, NHEADS, D_STATE)
        C_state = jnp.broadcast_to(C_state[:, :, :, None, :], (Bsz, L, NGROUPS, rep, D_STATE)).reshape(Bsz, L, NHEADS, D_STATE)
        A = -jnp.exp(A_log)
        y, _ = ssd_minimal_discrete(x_inner * dt[..., None], A[None, None, :] * dt, B_state, C_state, CHUNK)
        y = y + x_inner * D_param[None, None, :, None]
        y = y.reshape(Bsz, L, D_INNER)
        mu = jnp.mean(y, axis=-1, keepdims=True)
        var = jnp.mean((y - mu) ** 2, axis=-1, keepdims=True)
        y = (y - mu) * jax.lax.rsqrt(var + 1e-05) * gamma + beta
        y = y * jax.nn.silu(z)
        y = y @ W_out
        return y.reshape(Bsz, H, W, D_MODEL)

    def _gn(v, G=32, eps=1e-5):
        B_, H_, W_, C_ = v.shape
        g = v.reshape(B_, H_, W_, G, C_ // G)
        m = jnp.mean(g, axis=(1, 2, 4), keepdims=True)
        s = jnp.var(g, axis=(1, 2, 4), keepdims=True)
        return ((g - m) / jnp.sqrt(s + eps)).reshape(v.shape)

    def _ln_c(v, eps=1e-6):
        m = jnp.mean(v, axis=-1, keepdims=True)
        s = jnp.var(v, axis=-1, keepdims=True)
        return (v - m) / jnp.sqrt(s + eps)

    def _ln_t(v, eps=1e-5):
        m = jnp.mean(v, axis=-1, keepdims=True)
        s = jnp.var(v, axis=-1, keepdims=True)
        return (v - m) / jnp.sqrt(s + eps)

    def _to_tokens(v):
        B_, H_, W_, C_ = v.shape
        return v.reshape(B_, H_ * W_, C_)
    def _from_tokens(t, like):
        return t.reshape(like.shape)

    x = x + _L0_conv_ref(_gn(x), L0_conv_W_in, L0_conv_W_conv, L0_conv_b_conv, L0_conv_dt_bias, L0_conv_A_log, L0_conv_D_param, L0_conv_gamma, L0_conv_beta, L0_conv_W_out)
    return x


_drawn_inputs = setup_inputs


def setup_inputs(seed=0):
    import zlib

    import numpy as np

    out = dict(_drawn_inputs(seed))
    spreads = {'L0_conv_D_param': (1.0, 0.6), 'L0_conv_gamma': (1.0, 0.6), 'L0_conv_beta': (0.0, 0.698)}
    factors = {'L0_conv_b_conv': 5.786, 'L0_conv_dt_bias': 8.0, 'L0_conv_A_log': 8.0}
    for name, (base, spread) in spreads.items():
        noise = np.random.default_rng([zlib.crc32(name.encode()), seed]).standard_normal(out[name].shape)
        drawn = base * np.exp(spread * noise) if base else spread * noise
        out[name] = jnp.asarray(drawn.astype(out[name].dtype))
    for name, factor in factors.items():
        out[name] = (out[name] * factor).astype(out[name].dtype)
    return out
```

```python
from contextlib import ExitStack

import numpy as np
import concourse.bass as bass
from concourse import mybir

F32 = mybir.dt.float32
F32R = mybir.dt.float32r
ALU = mybir.AluOpType
ACT = mybir.ActivationFunctionType
AX = mybir.AxisListType

B, H, W, C = 8, 64, 64, 384
NG = 32
CG = C // NG
DI = 2 * C
NH, HD, NS = 12, 64, 16
PR = B // 2
TOK = B * W
KC = C // 128
MT = DI // 128
GR = NH // 4
BC = MT
B0, C0, DT0 = 0, 32, 64
BCP = C0 + NS
BCW = DT0 + NH
WIN = 2 * DI + BCW
GN_EPS, LN_EPS = 1e-5, 1e-5
SERIES = [1.0 / (2 * k + 1) for k in range(8)]

IDENT, LATER, UPTO, ONES, SAMEIMG, TRI, HEADOF, MHALF, LNEPS = 0, 128, 256, 384, 512, 544, 608, 612, 616
NCONST = 620


def constants():
    k = np.arange(128)[:, None]
    j = np.arange(128)[None, :]
    same = (k // W) == (j // W)
    c = np.zeros((128, NCONST), np.float32)
    c[:, IDENT:IDENT + 128] = k == j
    c[:, LATER:LATER + 128] = same & (k > j)
    c[:, UPTO:UPTO + 128] = same & (k <= j)
    c[:, ONES:ONES + 128] = 1.0
    c[:, SAMEIMG:SAMEIMG + 32] = (k // W) == (np.arange(32)[None, :] // NS)
    c[:, TRI:TRI + 64] = (k % W) <= np.arange(64)[None, :]
    c[:, HEADOF:HEADOF + 4] = (k // 32) == np.arange(4)[None, :]
    c[:, MHALF:MHALF + 4] = -0.5
    c[:, LNEPS:LNEPS + 4] = LN_EPS
    return c


class Row:

    def __init__(self, i, j):
        self.i, self.j = i, j

    def back(self, lag):
        return Row(self.i, self.j - lag)

    @property
    def parity(self):
        return self.j % 2

    @property
    def static(self):
        return isinstance(self.i, int)

    def exists(self):
        return not self.static or 0 <= 2 * self.i + self.j < H

    def number(self):
        return self.i * 2 + self.j

    def count(self, per_row, k):
        return self.i * (2 * per_row) + (self.j * per_row + k)

    def count_half(self, per_row, k):
        return self.i * per_row + ((self.j // 2) * per_row + k)


PER_ROW = dict(
    z_mm=6, yT_mm=6, xT_mm=3, cv_mm=7, out_mm=4, dtT_mm=1, bcg_mm=1, se_mm=1, xk_mm=6, df_mm=6,
    cet_mm=3, y_mm=3, st_mm=3,
    sz=6, ya=6, xh=3, dtv=1, du=2, de=1, bc_act=2, xc_act=6, xk=6, L=6, cet=3, sbd=3,
    yp=6, xl=3, tap=63, dch=16, gb=3, Mv=6, yv=6, bst=12, ss=6, agg=4, yn=4, ot=4,
    xn=2, R=3, be=3, ce=3, xd=3, xD=3, rs=2,
)

FILLS = []
def _fill(name, n, lag, sem, k):
    FILLS.append((name, n, lag, sem, k))
for _m in (0, 1, 2):
    _fill("z", _m, 2, "sz", _m + 1)
for _m in range(3):
    _fill("yT", _m, 2, "ya", _m + 1)
    _fill("z", _m + 3, 2, "sz", _m + 4)
for _m in (3, 4, 5):
    _fill("yT", _m, 2, "ya", _m + 1)
for _k in range(KC):
    _fill("xT", _k, 0, "xl", _k + 1)
_fill("out", 0, 2, "ot", 1)
_fill("se", 0, 1, "de", 1)
_fill("bcg", 0, 1, "gb", 3)
_fill("out", 1, 2, "ot", 2)
_fill("xk", 0, 1, "xk", 1)
_fill("out", 2, 2, "ot", 3)
_fill("xk", 1, 1, "xk", 2)
_fill("df", 0, 1, "L", 1)
_fill("df", 1, 1, "L", 2)
_fill("cet", 0, 1, "cet", 1)
_fill("st", 0, 1, "ss", 2)
_fill("xk", 2, 1, "xk", 3)
_fill("dtT", 0, 0, "dch", 1)
_fill("xk", 3, 1, "xk", 4)
_fill("df", 2, 1, "L", 3)
_fill("df", 3, 1, "L", 4)
_fill("cet", 1, 1, "cet", 2)
_fill("st", 1, 1, "ss", 4)
_fill("out", 3, 2, "ot", 4)
_fill("xk", 4, 1, "xk", 5)
_fill("xk", 5, 1, "xk", 6)
_fill("df", 4, 1, "L", 5)
_fill("df", 5, 1, "L", 6)
_fill("cet", 2, 1, "cet", 3)
_fill("st", 2, 1, "ss", 6)
PLACE = {(f[0], f[1]): n for n, f in enumerate(FILLS)}
assert len(FILLS) % 4 == 0


def build(nc, x, W_in, W_conv, b_conv_x, b_conv_bc, dt_bias, A_log, D_param, gamma, beta, W_out, consts, out):
    with ExitStack() as ctx:
        def sb(name, shape, dt=F32):
            return ctx.enter_context(nc.sbuf_tensor(name, shape, dt))

        def ps(name, shape=(128, 512)):
            return ctx.enter_context(nc.psum_tensor(name, list(shape), F32))

        def semaphore(name):
            return ctx.enter_context(nc.semaphore(name))

        cst = sb("cst", [128, NCONST])
        win_hi = sb("win_hi", [128, KC, WIN], F32R)
        win_lo = sb("win_lo", [128, KC, WIN], F32R)
        wout = sb("wout", [128, MT, C])
        wcv = sb("wcv", [128, MT, 9])
        wcv_bc = sb("wcv_bc", [BCP, 9])
        bcv = sb("bcv", [128, MT])
        bcv_bc = sb("bcv_bc", [BCP, 1])
        gam = sb("gam", [128, MT])
        bet = sb("bet", [128, MT])
        dtb = sb("dtb", [128, NH])
        negA = sb("negA", [128, NH])
        Dp = sb("Dp", [128, NH])
        gn_s = sb("gn_s", [128, PR * NG])
        gn_t = sb("gn_t", [128, PR * NG])
        xt = sb("xt", [128, 2, PR, C])
        xhi = sb("xhi", [128, 2, KC, TOK], F32R)
        xlo = sb("xlo", [128, 2, KC, TOK], F32R)
        acc = sb("acc", [128, 2, MT, TOK])
        acc_bc = sb("acc_bc", [BCP, 2, TOK])
        xc = sb("xc", [128, 2, TOK])
        xc_bc = sb("xc_bc", [BCP, TOK])
        bcB = sb("bcB", [NS, TOK])
        bcC = sb("bcC", [NS, TOK])
        dtv = sb("dtv", [NH, TOK])
        sm = sb("sm", [128, 9, PR * NH])
        dt = sb("dt", [128, 2, PR, NH])
        dA = sb("dA", [128, 2, PR, NH])
        DE = sb("DE", [128, 108])
        G = sb("G", [128, PR, W])
        Bbd = sb("Bbd", [128, PR, 2, NS])
        Cbd = sb("Cbd", [128, PR, 2, NS])
        R = sb("R", [128, PR, 4, W])
        L = sb("L", [128, PR, 4, W])
        BE = sb("BE", [128, PR, 4, 2 * NS])
        CE = sb("CE", [128, PR, 4, 2 * NS])
        CET = sb("CET", [128, PR, 128])
        S = sb("S", [128, GR, PR, HD])
        Sbd = sb("Sbd", [128, PR, 4, HD])
        Xtok = sb("Xtok", [128, 2, PR, 4 * HD])
        Xd = sb("Xd", [128, 2, PR, 4 * HD])
        y = sb("y", [128, PR, DI])
        bst = sb("bst", [128, PR, GR, 6])
        mv = sb("mv", [128, PR, 2])
        vare = sb("vare", [128, PR])
        rstd = sb("rstd", [128, PR])
        sz = sb("sz", [128, 3, TOK])
        ya = sb("ya", [128, 2, TOK])
        yprime = sb("yprime", [128, MT, TOK])
        xres = sb("xres", [128, 2, C])

        shared = [ps(f"shared{n}") for n in range(4)]
        cbank = [ps(f"conv{n}") for n in range(2)]
        ybank = [ps(f"ybank{n}") for n in range(2)]

        ident = cst[:, IDENT:IDENT + 128]
        tri = cst[:, TRI:TRI + W]
        sameimg = cst[:, SAMEIMG:SAMEIMG + 32]

        sem = {name: semaphore(name) for name in PER_ROW}
        s_const = semaphore("s_const")
        s_wst = semaphore("s_wst")
        s_wsplit = semaphore("s_wsplit")
        s_prep = semaphore("s_prep")
        s_init = semaphore("s_init")
        s_chunk = [semaphore("s_chunk0"), semaphore("s_chunk1")]
        s_sqr = semaphore("s_sqr")
        s_red = semaphore("s_red")
        s_var = semaphore("s_var")
        s_sum = semaphore("s_sum")
        s_pow = semaphore("s_pow")
        s_gn = semaphore("s_gn")
        s_last = semaphore("s_last")
        s_xin = [semaphore("s_xin0"), semaphore("s_xin1")]
        s_xr = [semaphore("s_xr0"), semaphore("s_xr1")]
        s_st = [semaphore("s_st0"), semaphore("s_st1")]

        def wait(eng, name, row, k):
            v = row.count(PER_ROW[name], k)
            if isinstance(v, int) and v <= 0:
                return
            eng.wait_ge(sem[name], v)

        def stand_alone(eng):
            eng.wait_ge(s_const, 16)

        def wait_half(eng, s, row, per_row, k):
            v = row.count_half(per_row, k)
            if isinstance(v, int) and v <= 0:
                return
            eng.wait_ge(s, v)

        def wait_free(eng, t, name, n):
            at = PLACE[name, n]
            place, back = at - 4, 0
            while back < 4:
                if place < 0:
                    place, back = place + len(FILLS), back + 1
                _, _, lag, reader, k = FILLS[place]
                row = t.back(back + lag)
                if row.exists():
                    wait(eng, reader, row, k)
                    break
                place -= 4
            return shared[at % 4]

        def bank_of(name, n):
            return shared[PLACE[name, n] % 4]

        def conv_bank(t, tile):
            o = 0 if tile == BC else tile + 1
            return cbank[(t.parity + o) % 2]

        def steps(eng):
            for t in range(4):
                yield Row(t // 2, t % 2)
            with eng.Fori(2, 31) as i:
                for j in range(2):
                    yield Row(i, j)
            for t in (62, 63, 64, 65):
                yield Row(t // 2, t % 2)

        NCHUNK, CTOK = 4, 8
        stage = [y[:, :, :].rearrange("p a b -> p (a b)"), yprime[:, :, :].rearrange("p a b -> p (a b)")]
        squares = acc[:, 0, :, :].rearrange("p a b -> p (a b)")
        sq_part = sm[:, 0:3, :].rearrange("p a b -> p (a b)")[:, 0:NCHUNK * NG].rearrange("p (c g) -> p c g", g=NG)
        gnw = R[:, :, :, :].rearrange("p a b c -> p (a b c)")
        sq_sum, ex, ex2, var, rs_g = (gnw[:, n * NG:(n + 1) * NG] for n in range(5))
        veps = gnw[:, 5 * NG:6 * NG]
        mhalf32 = gnw[:, 6 * NG:7 * NG]
        s8 = gnw[:, 256:512]
        t8 = gnw[:, 512:768]
        wst = [acc[:, 0, :, :].rearrange("p a b -> p (a b)"), acc[:, 1, :, :].rearrange("p a b -> p (a b)")]

        block = ctx.enter_context(nc.Block())

        @block.sync
        def _(sp):
            sp.dma_start(cst[:, :], consts[:, :]).then_inc(s_const, 16)
            for k in range(2):
                sp.dma_start(wst[k][:, 0:W_in.shape[1]], W_in[128 * k:128 * k + 128, :]).then_inc(s_wst, 16)
            sp.dma_start(wout[:, :, :], W_out.rearrange("(m p) n -> p m n", p=128)).then_inc(s_const, 16)
            sp.dma_start(wcv[:, :, :], W_conv[0:DI, :].rearrange("(m p) k -> p m k", p=128)).then_inc(s_const, 16)
            sp.dma_start(bcv[:, :], b_conv_x[:, :]).then_inc(s_const, 16)
            sp.wait_ge(s_init, 2)
            for at, n in ((B0, DI), (C0, DI + NS)):
                sp.dma_start(wcv_bc[at:at + NS, :], W_conv[n:n + NS, :]).then_inc(s_const, 16)
                sp.dma_start(bcv_bc[at:at + NS, :], b_conv_bc[n - DI:n - DI + NS, :]).then_inc(s_const, 16)
            sp.dma_start(gam[:, :], gamma[:, :]).then_inc(s_const, 16)
            sp.dma_start(bet[:, :], beta[:, :]).then_inc(s_const, 16)
            for dst, v in ((dtb, dt_bias), (negA, A_log), (Dp, D_param)):
                sp.dma_start(dst[:, :], v.rearrange("(a h) -> a h", a=1).to_broadcast([128, NH])).then_inc(s_const, 16)
            sp.wait_ge(s_wsplit, 8)
            sp.dma_start(wst[0][:, 0:W_in.shape[1]], W_in[256:384, :]).then_inc(s_wst, 16)

            xi = x.rearrange("b h w c -> b (h w c)").rearrange("b (p n) -> b p n", p=128)

            def image_chunks(im):
                for c in range(NCHUNK):
                    n = im * NCHUNK + (c - 2)
                    if n >= 0:
                        sp.wait_ge(s_sqr, n + 1)
                        sp.wait_ge(s_sum, im * (NCHUNK + 1) + (c - 1 if c >= 2 else c - 2))
                    src = xi[im, :, c * CTOK * C:(c + 1) * CTOK * C]
                    sp.dma_start(stage[c % 2][:, :], src).then_inc(s_chunk[c % 2], 16)

            for im in range(B):
                image_chunks(im)

            xpair = x.rearrange("(p i) h w c -> i h w p c", i=2)
            opair = out.rearrange("(p i) h w c -> i h w p c", i=2)

            def row_of(v, i, row):
                return v[i][bass.ds(row.number(), 1)].rearrange("a w p c -> w (a p) c")

            def load_row(row):
                for i in range(2):
                    sp.dma_start(xt[64 * i:64 * i + 64, row.parity], row_of(xpair, i, row)).then_inc(s_xin[row.parity], 16)

            def load_residual(row, p):
                v = row.count(64, 32 * (p // 2))
                if not (isinstance(v, int) and v <= 0):
                    sp.wait_ge(s_st[p % 2], v)
                for i in range(2):
                    sp.dma_start(xres[64 * i:64 * i + 64, p % 2], row_of(xpair, i, row)[:, p]).then_inc(s_xr[p % 2], 16)

            load_row(Row(0, 0))
            for t in steps(sp):
                if t.back(-1).exists() or not t.static:
                    wait(sp, "xT_mm", t.back(1), 3)
                    if not (t.static and 2 * t.i + t.j + 1 >= H):
                        load_row(t.back(-1))
                u = t.back(2)
                if u.exists():
                    for p in range(2):
                        load_residual(u, p)
                    for p in range(PR):
                        wait(sp, "ot", u, p + 1)
                        for i in range(2):
                            sp.dma_start(row_of(opair, i, u)[:, p], xres[64 * i:64 * i + 64, p % 2]).then_inc(s_st[p % 2], 16)
                        if p < 2:
                            load_residual(u, p + 2)
            for s in range(2):
                sp.wait_ge(s_st[s], 64 * H)

        @block.gpsimd
        def _(pool):
            pool.memset(mhalf32, -0.5).then_inc(s_pow, 1)

            def image_pow(im):
                pool.wait_ge(s_red, im * 9 + 8)
                if isinstance(im, int):
                    pool.wait_ge(s_pow, 1)
                pool.tensor_tensor(rs_g, veps, mhalf32, ALU.pow).then_inc(s_pow, 1)

            image_pow(0)
            with pool.Fori(1, B) as im:
                image_pow(im)

            pool.wait_ge(s_const, 16 * 13)
            pool.wait_ge(s_prep, 2)
            pool.wait_ge(s_gn, 4)
            pool.wait_ge(s_init, 12)

            def normalise(row):
                v = xt[:, row.parity].rearrange("p a (g c) -> p (a g) c", c=CG)
                wait_half(pool, s_xin[row.parity], row, 32, 32)
                pool.tensor_tensor(v, v, gn_s[:, :].unsqueeze(2).to_broadcast([128, PR * NG, CG]), ALU.mult).then_inc(sem["xn"], 1)
                wait(pool, "xn", row, 1)
                pool.tensor_tensor(v, v, gn_t[:, :].unsqueeze(2).to_broadcast([128, PR * NG, CG]), ALU.add).then_inc(sem["xn"], 1)

            def decay_steps(r, g):
                wait(pool, "dch", r, 16)
                wait(pool, "df_mm", r, 2 * g)
                a = dA[:, r.parity, :, 4 * g:4 * g + 4].unsqueeze(3).to_broadcast([128, PR, 4, W])
                m = tri.unsqueeze(1).unsqueeze(1).to_broadcast([128, PR, 4, W])
                pool.tensor_tensor(R[:, :, :, :], a, m, ALU.mult).then_inc(sem["R"], 1)

            def scale_BC(r, g):
                if g == 0:
                    wait(pool, "gb", r, 3)
                    wait(pool, "de", r, 1)
                d = DE[:, 0:96].rearrange("p (e a h) -> p e a h", e=2, a=PR)
                for name, dst, src, e, reader in (("be", BE, Bbd, 0, "st_mm"), ("ce", CE, Cbd, 1, "cet_mm")):
                    wait(pool, reader, r, g)
                    v = src[:, :, :, :].rearrange("p a i n -> p a (i n)").unsqueeze(2).to_broadcast([128, PR, 4, 2 * NS])
                    w = d[:, e, :, 4 * g:4 * g + 4].unsqueeze(3).to_broadcast([128, PR, 4, 2 * NS])
                    pool.tensor_tensor(dst[:, :, :, :], v, w, ALU.mult).then_inc(sem[name], 1)

            def scale_x(r, g):
                slot = (r.parity + g) % 2
                xv = Xtok[:, slot].rearrange("p a (h d) -> p a h d", h=4)
                wait(pool, "xk", r, 2 * g + 2)
                wait(pool, "st_mm", r, g - 1)
                w = dt[:, r.parity, :, 4 * g:4 * g + 4].unsqueeze(3).to_broadcast([128, PR, 4, HD])
                pool.tensor_tensor(Xd[:, slot].rearrange("p a (h d) -> p a h d", h=4), xv, w, ALU.mult).then_inc(sem["xd"], 1)
                w = Dp[:, 4 * g:4 * g + 4].unsqueeze(1).unsqueeze(3).to_broadcast([128, PR, 4, HD])
                pool.tensor_tensor(xv, xv, w, ALU.mult).then_inc(sem["xD"], 1)

            normalise(Row(0, 0))
            for t in steps(pool):
                r = t.back(1)
                if r.exists():
                    decay_steps(r, 0)
                    scale_BC(r, 0)
                if not (t.static and 2 * t.i + t.j + 1 >= H):
                    normalise(t.back(-1))
                if r.exists():
                    scale_x(r, 0)
                    for g in (1, 2):
                        decay_steps(r, g)
                        scale_BC(r, g)
                        scale_x(r, g)
                    wait(pool, "agg", r, 4)
                    pool.tensor_tensor(vare[:, :], mv[:, :, 1], cst[:, LNEPS:LNEPS + PR], ALU.add).then_inc(sem["rs"], 1)
                    wait(pool, "rs", r, 1)
                    pool.tensor_tensor(rstd[:, :], vare[:, :], cst[:, MHALF:MHALF + PR], ALU.pow).then_inc(sem["rs"], 1)

        @block.scalar
        def _(act):
            act.wait_ge(s_const, 16 * 13)
            act.activation(negA[:, :], negA[:, :], ACT.Exp).then_inc(s_prep, 1)
            act.wait_ge(s_prep, 1)
            act.mul(negA[:, :], negA[:, :], -1.0).then_inc(s_prep, 1)
            act.wait_ge(s_wsplit, 3 * 8)

            def image_squares(im):
                for c in range(NCHUNK):
                    act.wait_ge(s_chunk[c % 2], (im * (NCHUNK // 2) + (c // 2 + 1)) * 16)
                    if not (isinstance(im, int) and im == 0 and c == 0):
                        act.wait_ge(s_red, im * 9 + (c if c else -4))
                    act.activation(squares, stage[c % 2], ACT.Square).then_inc(s_sqr, 1)

            image_squares(0)
            with act.Fori(1, B) as im:
                image_squares(im)

            def gate(u, m):
                wait(act, "z_mm", u, m + 1)
                wait(act, "yp", u, m - 2)
                act.activation(sz[:, m % 3], bank_of("z", m)[:, :], ACT.Silu).then_inc(sem["sz"], 1)

            def affine(u, m):
                wait(act, "yT_mm", u, m + 1)
                wait(act, "yp", u, m - 1)
                act.activation(ya[:, m % 2], bank_of("yT", m)[:, :], ACT.Identity, bias=bet[:, m:m + 1],
                               scale=gam[:, m:m + 1]).then_inc(sem["ya"], 1)

            def x_hi(t, k):
                wait(act, "xT_mm", t, k + 1)
                wait(act, "z_mm", t.back(2), 6)
                act.activation(xhi[:, t.parity, k], bank_of("xT", k)[:, :], ACT.Copy).then_inc(sem["xh"], 1)

            def silu_conv(r, j):
                t = r.back(-1)
                if t.static and 2 * t.i + t.j == H:
                    act.wait_ge(s_last, j + 2)
                else:
                    wait(act, "tap", t, 9 * (j + 1) + 5)
                act.activation(xc[:, j % 2], xc[:, j % 2], ACT.Silu).then_inc(sem["xc_act"], 1)

            def take_xk(r, j):
                g = j // 2
                wait(act, "xk_mm", r, j + 1)
                wait(act, "yv", r, 2 * g - 2)
                src = bank_of("xk", j)[:, :].rearrange("p (a c) -> p a c", a=PR)
                act.activation(Xtok[:, (r.parity + g) % 2, :, 128 * (j % 2):128 * (j % 2) + 128], src,
                               ACT.Copy).then_inc(sem["xk"], 1)

            def state_blocks(r, g):
                wait(act, "ss", r.back(1), 2 * g + 2)
                wait(act, "y_mm", r, g)
                for h in range(4):
                    last = act.activation(Sbd[:, :, h], S[:, g], ACT.Copy, scale=cst[:, HEADOF + h:HEADOF + h + 1])
                last.then_inc(sem["sbd"], 1)

            def exp_decay(r, g):
                for b in range(2):
                    wait(act, "df_mm", r, 2 * g + b + 1)
                    wait(act, "y_mm", r, g)
                    src = bank_of("df", 2 * g + b)[:, :].rearrange("p (a h l) -> p a h l", a=2, h=4)
                    act.activation(L[:, 2 * b:2 * b + 2], src, ACT.Exp).then_inc(sem["L"], 1)

            def take_cet(r, g):
                wait(act, "cet_mm", r, g + 1)
                wait(act, "y_mm", r, g)
                act.activation(CET[:, :, :], bank_of("cet", g)[:, :].rearrange("p (a l) -> p a l", a=PR),
                               ACT.Copy).then_inc(sem["cet"], 1)

            act.wait_ge(s_init, 12)
            for t in steps(act):
                r, u = t.back(1), t.back(2)
                if u.exists():
                    for m in (0, 1, 2):
                        gate(u, m)
                    for m in range(3):
                        affine(u, m)
                        gate(u, m + 3)
                    for m in (3, 4, 5):
                        affine(u, m)
                if t.exists():
                    for k in range(KC):
                        x_hi(t, k)
                    wait(act, "cv_mm", t, 1)
                    wait(act, "dtT_mm", t, 0)
                    act.activation(dtv[:, :], conv_bank(t, BC)[DT0:DT0 + NH, :], ACT.Copy).then_inc(sem["dtv"], 1)
                if r.exists():
                    wait(act, "se_mm", r, 1)
                    wait(act, "ce", r, 0)
                    wait(act, "ss", r, 0)
                    act.activation(DE[:, :], bank_of("se", 0)[:, 0:108], ACT.Exp).then_inc(sem["de"], 1)
                    if t.static and 2 * t.i + t.j == H:
                        act.wait_ge(s_last, 1)
                    else:
                        wait(act, "tap", t, 5)
                    wait(act, "bcg_mm", r, 0)
                    act.activation(bcB[:, :], xc_bc[B0:B0 + NS, :], ACT.Silu).then_inc(sem["bc_act"], 1)
                    act.activation(bcC[:, :], xc_bc[C0:C0 + NS, :], ACT.Silu).then_inc(sem["bc_act"], 1)
                    state_blocks(r, 0)
                    silu_conv(r, 0)
                    take_xk(r, 0)
                    silu_conv(r, 1)
                    take_xk(r, 1)
                    exp_decay(r, 0)
                    take_cet(r, 0)
                    silu_conv(r, 2)
                    take_xk(r, 2)
                if t.exists():
                    wait(act, "dch", t, 1)
                    act.activation(sm[:, 1], sm[:, 0], ACT.Abs).then_inc(sem["du"], 1)
                    wait(act, "du", t, 1)
                    act.activation(sm[:, 2], sm[:, 1], ACT.Exp, scale=-1.0).then_inc(sem["du"], 1)
                if r.exists():
                    silu_conv(r, 3)
                    take_xk(r, 3)
                    state_blocks(r, 1)
                    exp_decay(r, 1)
                    take_cet(r, 1)
                    silu_conv(r, 4)
                    take_xk(r, 4)
                    silu_conv(r, 5)
                    take_xk(r, 5)
                    state_blocks(r, 2)
                    exp_decay(r, 2)
                    take_cet(r, 2)

        @block.vector
        def _(dve):
            dve.memset(wcv_bc[:, :], 0.0).then_inc(s_init, 1)
            dve.memset(bcv_bc[:, :], 0.0).then_inc(s_init, 1)
            for w in (win_hi, win_lo):
                dve.memset(w[:, :, 2 * DI:WIN].bitcast(F32), 0.0).then_inc(s_init, 1)
            dve.memset(S[:, :, :, :], 0.0).then_inc(s_init, 1)
            dve.wait_ge(s_init, 5)
            spans = [(0, 2 * DI, 0), (2 * DI, 2 * DI + NS, 2 * DI + B0), (2 * DI + NS, 2 * DI + 2 * NS, 2 * DI + C0),
                     (2 * DI + 2 * NS, 2 * DI + 2 * NS + NH, 2 * DI + DT0)]
            for k, slot in ((0, 0), (1, 1), (2, 0)):
                dve.wait_ge(s_wst, 48 if k == 2 else 32)
                for n, (a, b, at) in enumerate(spans):
                    dve.tensor_copy(win_hi[:, k, at:at + b - a], wst[slot][:, a:b]).then_inc(s_wsplit, 1)
                dve.wait_ge(s_wsplit, 8 * k + 4)
                for n, (a, b, at) in enumerate(spans):
                    dve.tensor_tensor(win_lo[:, k, at:at + b - a], wst[slot][:, a:b],
                                      win_hi[:, k, at:at + b - a].bitcast(F32), ALU.subtract).then_inc(s_wsplit, 1)

            dve.wait_ge(s_const, 16 * 13)

            def image_stats(im):
                for c in range(NCHUNK):
                    dve.wait_ge(s_sqr, im * NCHUNK + (c + 1))
                    if c == 0 and not isinstance(im, int):
                        dve.wait_ge(s_sum, im * (NCHUNK + 1))
                    dve.tensor_reduce(sq_part[:, c], squares.rearrange("p (n g c) -> p g n c", g=NG, c=CG), AX.XY,
                                      ALU.add).then_inc(s_red, 1)
                dve.wait_ge(s_red, im * 9 + 4)
                dve.tensor_reduce(sq_sum, sq_part.rearrange("p c g -> p g c"), AX.X, ALU.add).then_inc(s_red, 1)
                dve.wait_ge(s_sum, im * (NCHUNK + 1) + (NCHUNK + 1))
                dve.tensor_reduce(ex, cbank[0][:, 0:C].rearrange("p (g c) -> p g c", c=CG), AX.X, ALU.add).then_inc(s_red, 1)
                dve.tensor_scalar(ex2, cbank[1][:, 0:NG], 1.0 / (H * W * CG), GN_EPS, ALU.mult, ALU.add).then_inc(s_red, 1)
                dve.wait_ge(s_red, im * 9 + 7)
                dve.scalar_tensor_tensor(out=var, in0=ex, scalar=-1.0 / (H * W * CG) ** 2, in1=ex, op0=ALU.mult,
                                         op1=ALU.mult).then_inc(s_var, 1)
                dve.wait_ge(s_var, im * 3 + 1)
                dve.tensor_tensor(veps, ex2, var, ALU.add).then_inc(s_red, 1)
                dve.wait_ge(s_pow, im + 2)
                dve.tensor_copy(s8[:, bass.ts(im, NG)], rs_g).then_inc(s_var, 1)
                dve.scalar_tensor_tensor(out=t8[:, bass.ts(im, NG)], in0=ex, scalar=-1.0 / (H * W * CG), in1=rs_g,
                                         op0=ALU.mult, op1=ALU.mult).then_inc(s_var, 1)
                dve.wait_ge(s_var, im * 3 + 3)
                dve.tensor_copy(ex2[:, 0:1], ex2[:, 0:1]).then_inc(s_red, 1)

            image_stats(0)
            with dve.Fori(1, B) as im:
                image_stats(im)
            dve.wait_ge(s_var, 3 * B)
            for dst, src in ((gn_s, s8), (gn_t, t8)):
                v = src.rearrange("p (a i g) -> p a i g", i=2, g=NG)
                for i in range(2):
                    dve.tensor_copy(dst[64 * i:64 * i + 64, :].rearrange("p (a g) -> p a g", g=NG),
                                    v[64 * i:64 * i + 64, :, i]).then_inc(s_gn, 1)

            dve.memset(acc[:, 1], 0.0).then_inc(s_init, 1)
            dve.memset(acc_bc[:, 1], 0.0).then_inc(s_init, 1)
            dve.wait_ge(s_init, 7)
            for m in range(MT):
                ins = dve.tensor_scalar(acc[:, 0, m], acc[:, 1, m], bcv[:, m:m + 1], None, ALU.add)
                if m < MT - 2:
                    ins.then_inc(s_init, 1)
            dve.tensor_scalar(acc_bc[:, 0], acc_bc[:, 1], bcv_bc[:, 0:1], None, ALU.add).then_inc(s_init, 1)
            dve.wait_ge(s_init, 12)

            def conv(t, tile, between=None):
                o = 0 if tile == BC else tile + 1
                bank = conv_bank(t, tile)
                if tile == BC:
                    src, done, this, w, bias = bank[0:BCP, :], acc_bc[:, (t.parity + 1) % 2], acc_bc[:, t.parity], wcv_bc, bcv_bc[:, 0:1]
                    dst, tap = xc_bc[:, :], lambda ky, kx: w[:, 3 * ky + kx:3 * ky + kx + 1]
                else:
                    src, done, this, w, bias = bank[:, :], acc[:, (t.parity + 1) % 2, tile], acc[:, t.parity, tile], wcv, bcv[:, tile:tile + 1]
                    dst, tap = xc[:, tile % 2], lambda ky, kx: w[:, tile, 3 * ky + kx:3 * ky + kx + 1]
                s3, d3, a3 = (v.rearrange("p (b w) -> p b w", w=W) for v in (src, done, this))
                begun = d3

                def left(a, ky):
                    return dve.scalar_tensor_tensor(out=a[:, :, 1:W], in0=s3[:, :, 0:W - 1], scalar=tap(ky, 0),
                                                    in1=a[:, :, 1:W], op0=ALU.mult, op1=ALU.add)

                def right(a, ky):
                    return dve.scalar_tensor_tensor(out=a[:, :, 0:W - 1], in0=s3[:, :, 1:W], scalar=tap(ky, 2),
                                                    in1=a[:, :, 0:W - 1], op0=ALU.mult, op1=ALU.add)

                def fill(n):
                    if between is not None:
                        between(n)

                wait(dve, "cv_mm", t, o + 1)
                wait(dve, "tap", t.back(1), 9 * o + 9)
                left(d3, 2).then_inc(sem["tap"], 1)
                fill(0)
                left(a3, 1).then_inc(sem["tap"], 1)
                fill(1)
                wait(dve, "tap", t, 9 * o + 1)
                right(d3, 2).then_inc(sem["tap"], 1)
                fill(2)
                wait(dve, "tap", t, 9 * o + 2)
                right(a3, 1).then_inc(sem["tap"], 1)
                fill(3)
                if tile == BC:
                    wait(dve, "bc_act", t.back(1), 0)
                else:
                    wait(dve, "xk_mm", t.back(1), tile - 1)
                wait(dve, "tap", t, 9 * o + 3)
                dve.scalar_tensor_tensor(out=dst, in0=src, scalar=tap(2, 1), in1=done, op0=ALU.mult,
                                         op1=ALU.add).then_inc(sem["tap"], 1)
                fill(4)
                wait(dve, "tap", t, 9 * o + 4)
                dve.scalar_tensor_tensor(out=this, in0=src, scalar=tap(1, 1), in1=this, op0=ALU.mult,
                                         op1=ALU.add).then_inc(sem["tap"], 1)
                fill(5)
                wait(dve, "tap", t, 9 * o + 5)
                dve.tensor_scalar(done, src, tap(0, 1), bias, ALU.mult, ALU.add).then_inc(sem["tap"], 1)
                fill(6)
                wait(dve, "tap", t, 9 * o + 7)
                left(begun, 0).then_inc(sem["tap"], 1)
                fill(7)
                wait(dve, "tap", t, 9 * o + 8)
                right(begun, 0).then_inc(sem["tap"], 1)
                fill(8)

            def last_row(r, tile):
                wait(dve, "tap", r, 63)
                if tile == BC:
                    wait(dve, "bc_act", r, 0)
                    dve.tensor_copy(xc_bc[:, :], acc_bc[:, r.parity]).then_inc(s_last, 1)
                else:
                    wait(dve, "xk_mm", r, tile - 1)
                    dve.tensor_copy(xc[:, tile % 2], acc[:, r.parity, tile]).then_inc(s_last, 1)

            def conv_tile(t, tile, between=None):
                if t.exists():
                    conv(t, tile, between)
                elif t.back(1).exists():
                    last_row(t.back(1), tile)

            def softplus_step(t, n):
                v, u, w2, rw, q, s, p, lp, vr = (sm[:, n_] for n_ in (0, 2, 3, 4, 5, 6, 7, 8, 1))
                d = dt[:, t.parity].rearrange("p a h -> p (a h)")

                def done(ins):
                    ins.then_inc(sem["dch"], 1)

                if n == 1:
                    wait(dve, "du", t, 2)
                else:
                    wait(dve, "dch", t, n)
                if n == 1:
                    done(dve.tensor_scalar(w2, u, 2.0, None, ALU.add))
                elif n == 2:
                    done(dve.reciprocal(rw, w2))
                elif n == 3:
                    done(dve.tensor_tensor(q, u, rw, ALU.mult))
                elif n == 4:
                    done(dve.tensor_tensor(s, q, q, ALU.mult))
                elif n == 5:
                    done(dve.tensor_scalar(p, s, SERIES[7], None, ALU.mult))
                elif n <= 11:
                    done(dve.scalar_tensor_tensor(out=p, in0=p, scalar=SERIES[12 - n], in1=s, op0=ALU.add, op1=ALU.mult))
                elif n == 12:
                    done(dve.scalar_tensor_tensor(out=lp, in0=p, scalar=1.0, in1=q, op0=ALU.add, op1=ALU.mult))
                elif n == 13:
                    done(dve.tensor_scalar(vr, v, 0.0, None, ALU.max))
                elif n == 14:
                    wait(dve, "xd", t.back(1), 0)
                    wait(dve, "se_mm", t.back(1), 0)
                    done(dve.scalar_tensor_tensor(out=d, in0=lp, scalar=2.0, in1=vr, op0=ALU.mult, op1=ALU.add))
                elif n == 15:
                    done(dve.tensor_tensor(dA[:, t.parity], dt[:, t.parity],
                                           negA[:, :].unsqueeze(1).to_broadcast([128, PR, NH]), ALU.mult))

            def residual(u, p):
                wait(dve, "out_mm", u, p + 1)
                dve.wait_ge(s_xr[p % 2], u.count(64, 32 * (p // 2) + 32))
                dve.tensor_tensor(xres[:, p % 2], bank_of("out", p)[:, 0:C], xres[:, p % 2], ALU.add).then_inc(sem["ot"], 1)

            def masked(r, g):
                for b in range(2):
                    wait(dve, "L", r, 2 * g + b + 1)
                    wait(dve, "gb", r, 1)
                    v = L[:, 2 * b:2 * b + 2]
                    dve.tensor_tensor(v, v, G[:, 2 * b:2 * b + 2].unsqueeze(2).to_broadcast([128, 2, 4, W]),
                                      ALU.mult).then_inc(sem["Mv"], 1)

            def take_y(r, g):
                slot = (r.parity + g) % 2
                wait(dve, "y_mm", r, g + 1)
                wait(dve, "xD", r, g + 1)
                wait(dve, "yT_mm", r.back(1), 6)
                for b in range(2):
                    dve.tensor_tensor(y[:, 2 * b:2 * b + 2, 256 * g:256 * g + 256],
                                      ybank[b][:, :].rearrange("p (a c) -> p a c", a=2),
                                      Xtok[:, slot, 2 * b:2 * b + 2], ALU.add).then_inc(sem["yv"], 1)
                for p in range(PR):
                    wait(dve, "yv", r, 2 * g + 1 + p // 2)
                    dve.bn_stats(bst[:, p, g], y[:, p, 256 * g:256 * g + 256]).then_inc(sem["bst"], 1)

            def new_state(r, g):
                wait(dve, "sbd", r, g + 1)
                wait(dve, "de", r, 1)
                dec = DE[:, 96:108].rearrange("p (a g) -> p a g", a=PR)[:, :, g].unsqueeze(2).to_broadcast([128, PR, HD])
                dve.tensor_tensor(S[:, g], S[:, g], dec, ALU.mult).then_inc(sem["ss"], 1)
                wait(dve, "st_mm", r, g + 1)
                wait(dve, "ss", r, 2 * g + 1)
                dve.tensor_tensor(S[:, g], bank_of("st", g)[:, 0:256].rearrange("p (a d) -> p a d", a=PR), S[:, g],
                                  ALU.add).then_inc(sem["ss"], 1)

            for t in steps(dve):
                r, u = t.back(1), t.back(2)
                if u.exists():
                    for m in range(MT):
                        wait(dve, "sz", u, m + 1)
                        wait(dve, "ya", u, m + 1)
                        wait(dve, "out_mm", u, 0)
                        dve.tensor_tensor(yprime[:, m], ya[:, m % 2], sz[:, m % 3], ALU.mult).then_inc(sem["yp"], 1)
                if t.exists():
                    for k in range(KC):
                        wait(dve, "xh", t, k + 1)
                        dve.tensor_tensor(xlo[:, t.parity, k], bank_of("xT", k)[:, :], xhi[:, t.parity, k].bitcast(F32),
                                          ALU.subtract).then_inc(sem["xl"], 1)
                conv_tile(t, BC)
                conv_tile(t, 0)
                if u.exists():
                    residual(u, 0)
                if r.exists():
                    wait(dve, "bcg_mm", r, 1)
                    wait(dve, "Mv", r, 0)
                    wait(dve, "ce", r, 0)
                    bank = bank_of("bcg", 0)
                    dve.tensor_tensor(G[:, :, :], bank[:, 0:256].rearrange("p (a l) -> p a l", a=PR),
                                      tri.unsqueeze(1).to_broadcast([128, PR, W]), ALU.mult).then_inc(sem["gb"], 1)
                    for n, dst in enumerate((Bbd, Cbd)):
                        v = bank[:, 256 + 64 * n:320 + 64 * n].rearrange("p (a n) -> p a n", a=PR).unsqueeze(2)
                        dve.tensor_tensor(dst[:, :, :, :], v.to_broadcast([128, PR, 2, NS]),
                                          sameimg.rearrange("p (i n) -> p i n", i=2).unsqueeze(1).to_broadcast([128, PR, 2, NS]),
                                          ALU.mult).then_inc(sem["gb"], 1)
                conv_tile(t, 1)
                if u.exists():
                    residual(u, 1)
                conv_tile(t, 2)
                if u.exists():
                    residual(u, 2)
                if r.exists():
                    masked(r, 0)
                conv_tile(t, 3)
                if r.exists():
                    take_y(r, 0)
                    new_state(r, 0)
                if t.exists():
                    wait(dve, "dtT_mm", t, 1)
                    dve.tensor_tensor(sm[:, 0].rearrange("p (a h) -> p a h", a=PR),
                                      bank_of("dtT", 0)[:, 0:PR * NH].rearrange("p (a h) -> p a h", a=PR),
                                      dtb[:, :].unsqueeze(1).to_broadcast([128, PR, NH]), ALU.add).then_inc(sem["dch"], 1)
                conv_tile(t, 4, lambda n: softplus_step(t, n) if n else None)
                if r.exists():
                    masked(r, 1)
                conv_tile(t, 5, lambda n: softplus_step(t, n + 9) if n < 7 else None)
                if r.exists():
                    take_y(r, 1)
                    new_state(r, 1)
                if u.exists():
                    residual(u, 3)
                if r.exists():
                    masked(r, 2)
                    take_y(r, 2)
                    wait(dve, "bst", r, 12)
                    new_state(r, 2)
                    for p in range(PR):
                        dve.bn_aggr(mv[:, p], bst[:, p].rearrange("p g s -> p (g s)")).then_inc(sem["agg"], 1)
                    wait(dve, "rs", r, 2)
                    for p in range(PR):
                        dve.tensor_scalar(y[:, p], y[:, p], mv[:, p, 0:1], rstd[:, p:p + 1], ALU.subtract,
                                          ALU.mult).then_inc(sem["yn"], 1)

        @block.tensor
        def _(pe):
            pe.wait_ge(s_const, 16 * 13)

            def image_sums(im):
                for c in range(NCHUNK):
                    pe.wait_ge(s_chunk[c % 2], (im * (NCHUNK // 2) + (c // 2 + 1)) * 16)
                    if c == 0 and not isinstance(im, int):
                        pe.wait_ge(s_red, im * 9)
                    for n in range(CTOK):
                        last = pe.matmul(cbank[0][:, 0:C], cst[:, ONES:ONES + 128], stage[c % 2][:, n * C:(n + 1) * C],
                                         start=(c == 0 and n == 0), stop=(c == NCHUNK - 1 and n == CTOK - 1))
                    last.then_inc(s_sum, 1)
                pe.wait_ge(s_red, im * 9 + 5)
                pe.matmul(cbank[1][:, 0:NG], cst[:, ONES:ONES + 128], sq_sum, start=True, stop=True).then_inc(s_sum, 1)

            image_sums(0)
            with pe.Fori(1, B) as im:
                image_sums(im)

            pe.wait_ge(s_wsplit, 24)
            pe.wait_ge(s_init, 12)

            def project(dst, col, par, width=128):
                n = 0
                for wt, xv in ((win_lo, xhi), (win_hi, xlo), (win_hi, xhi)):
                    for k in range(KC):
                        last = pe.matmul(dst, wt[:, k, col:col + width], xv[:, par, k], start=(n == 0), stop=(n == 3 * KC - 1))
                        n += 1
                return last

            def z_tile(t, m):
                u = t.back(2)
                bank = wait_free(pe, t, "z", m)
                project(bank[:, :], 128 * m, u.parity).then_inc(sem["z_mm"], 1)

            def y_transposed(t, m):
                u = t.back(2)
                bank = wait_free(pe, t, "yT", m)
                wait(pe, "yn", u, 4)
                for p in range(PR):
                    last = pe.transpose(bank[:, 128 * p:128 * p + 128], y[:, p, 128 * m:128 * m + 128], ident)
                last.then_inc(sem["yT_mm"], 1)

            def x_transposed(t, k):
                bank = wait_free(pe, t, "xT", k)
                wait(pe, "xn", t, 2)
                for p in range(PR):
                    last = pe.transpose(bank[:, 128 * p:128 * p + 128], xt[:, t.parity, p, 128 * k:128 * k + 128], ident)
                last.then_inc(sem["xT_mm"], 1)

            def conv_input(t, tile):
                o = 0 if tile == BC else tile + 1
                wait(pe, "tap", t, 9 * (o - 1))
                wait(pe, "xl", t, 3)
                if o in (1, 2):
                    wait(pe, "dtv", t, o - 1)
                if tile == BC:
                    last = project(conv_bank(t, tile)[0:BCW, :], 2 * DI, t.parity, BCW)
                else:
                    last = project(conv_bank(t, tile)[:, :], DI + 128 * tile, t.parity)
                last.then_inc(sem["cv_mm"], 1)

            def out_pair(t, p):
                u = t.back(2)
                bank = wait_free(pe, t, "out", p)
                wait(pe, "yp", u, 6)
                for m in range(MT):
                    last = pe.matmul(bank[:, 0:C], yprime[:, m, 128 * p:128 * p + 128], wout[:, m, :], start=(m == 0),
                                     stop=(m == MT - 1))
                last.then_inc(sem["out_mm"], 1)

            def decay_sums(t):
                r = t.back(1)
                bank = wait_free(pe, t, "se", 0)
                wait(pe, "dch", r, 16)
                a = dA[:, r.parity].rearrange("p a h -> p (a h)")
                pe.matmul(bank[:, 0:48], cst[:, LATER:LATER + 128], a, start=True, stop=True)
                pe.matmul(bank[:, 48:96], cst[:, UPTO:UPTO + 128], a, start=True, stop=True)
                for h in range(4):
                    rhs = dA[:, r.parity].rearrange("p a (g h) -> p a g h", h=4)[:, :, :, h]
                    last = pe.matmul(bank[32 * h:32 * h + 32, 96:108].rearrange("p (a g) -> p a g", a=PR), sameimg, rhs,
                                     start=True, stop=True)
                last.then_inc(sem["se_mm"], 1)

            def b_and_c(t):
                r = t.back(1)
                stand_alone(pe)
                bank = wait_free(pe, t, "bcg", 0)
                wait(pe, "bc_act", r, 2)
                for p in range(PR):
                    for i in range(2):
                        tok = slice(128 * p + 64 * i, 128 * p + 64 * i + 64)
                        pe.matmul(bank[64 * i:64 * i + 64, 64 * p:64 * p + 64], bcB[:, tok], bcC[:, tok], start=True, stop=True)
                for n, v in enumerate((bcB, bcC)):
                    for p in range(PR):
                        at = 256 + 64 * n + 16 * p
                        last = pe.transpose(bank[:, at:at + NS], v[:, 128 * p:128 * p + 128], cst[0:NS, IDENT:IDENT + NS])
                last.then_inc(sem["bcg_mm"], 1)

            def x_tokens(t, j):
                r = t.back(1)
                bank = wait_free(pe, t, "xk", j)
                wait(pe, "xc_act", r, j + 1)
                for p in range(PR):
                    last = pe.transpose(bank[:, 128 * p:128 * p + 128], xc[:, j % 2, 128 * p:128 * p + 128], ident)
                last.then_inc(sem["xk_mm"], 1)

            def decay_matrix(t, g):
                r = t.back(1)
                for b in range(2):
                    bank = wait_free(pe, t, "df", 2 * g + b)
                    wait(pe, "R", r, g + 1)
                    pe.matmul(bank[:, :], cst[:, LATER:LATER + 128], R[:, 2 * b:2 * b + 2].rearrange("p a h l -> p (a h l)"),
                              start=True, stop=True).then_inc(sem["df_mm"], 1)

            def c_channels(t, g):
                r = t.back(1)
                bank = wait_free(pe, t, "cet", g)
                wait(pe, "ce", r, g + 1)
                for p in range(PR):
                    last = pe.transpose(bank[:, 128 * p:128 * p + 128], CE[:, p].rearrange("p h n -> p (h n)"), ident)
                last.then_inc(sem["cet_mm"], 1)

            def scan_y(t, g):
                r = t.back(1)
                slot = (r.parity + g) % 2
                wait(pe, "yv", r, 2 * g)
                wait(pe, "cet", r, g + 1)
                wait(pe, "sbd", r, g + 1)
                for p in range(PR):
                    bank = ybank[p // 2]
                    pe.matmul(bank[:, 256 * (p % 2):256 * (p % 2) + 256], CET[:, p], Sbd[:, p].rearrange("p h d -> p (h d)"),
                              start=(p % 2 == 0), stop=False, skip_group_check=True)
                stand_alone(pe)
                wait(pe, "Mv", r, 2 * g + 2)
                wait(pe, "xd", r, g + 1)
                for h in range(4):
                    for q in range(2):
                        for i, b in ((0, 0), (1, 1), (0, 1), (1, 0)):
                            p = 2 * b + q
                            part = slice(64 * i, 64 * i + 64)
                            last = pe.matmul(ybank[b][part, 256 * q + 64 * h:256 * q + 64 * h + 64], L[part, p, h],
                                             Xd[part, slot, p, 64 * h:64 * h + 64], start=False, stop=True,
                                             skip_group_check=True)
                last.then_inc(sem["y_mm"], 1)

            def scan_state(t, g):
                r = t.back(1)
                slot = (r.parity + g) % 2
                bank = wait_free(pe, t, "st", g)
                wait(pe, "be", r, g + 1)
                wait(pe, "xd", r, g + 1)
                for p in range(PR):
                    for h in range(4):
                        last = pe.matmul(bank[32 * h:32 * h + 32, 64 * p:64 * p + 64], BE[:, p, h],
                                         Xd[:, slot, p, 64 * h:64 * h + 64], start=True, stop=True)
                last.then_inc(sem["st_mm"], 1)

            def dt_tokens(t):
                stand_alone(pe)
                bank = wait_free(pe, t, "dtT", 0)
                wait(pe, "dtv", t, 1)
                for p in range(PR):
                    last = pe.transpose(bank[:, NH * p:NH * p + NH], dtv[:, 128 * p:128 * p + 128], cst[0:NH, IDENT:IDENT + NH])
                last.then_inc(sem["dtT_mm"], 1)

            for t in steps(pe):
                r, u = t.back(1), t.back(2)
                ssd, tail, conv = r.exists(), u.exists(), t.exists()
                if tail:
                    for m in (0, 1, 2):
                        z_tile(t, m)
                    for m in range(3):
                        y_transposed(t, m)
                        z_tile(t, m + 3)
                    for m in (3, 4, 5):
                        y_transposed(t, m)
                if conv:
                    for k in range(KC):
                        x_transposed(t, k)
                    conv_input(t, BC)
                    conv_input(t, 0)
                if tail:
                    out_pair(t, 0)
                if ssd:
                    decay_sums(t)
                    b_and_c(t)
                if conv:
                    conv_input(t, 1)
                if tail:
                    out_pair(t, 1)
                if ssd:
                    x_tokens(t, 0)
                if conv:
                    conv_input(t, 2)
                if tail:
                    out_pair(t, 2)
                if ssd:
                    x_tokens(t, 1)
                    decay_matrix(t, 0)
                    c_channels(t, 0)
                if conv:
                    conv_input(t, 3)
                if ssd:
                    scan_y(t, 0)
                    scan_state(t, 0)
                    x_tokens(t, 2)
                if conv:
                    dt_tokens(t)
                    conv_input(t, 4)
                if ssd:
                    x_tokens(t, 3)
                    decay_matrix(t, 1)
                    c_channels(t, 1)
                if conv:
                    conv_input(t, 5)
                if ssd:
                    scan_y(t, 1)
                    scan_state(t, 1)
                if tail:
                    out_pair(t, 3)
                if ssd:
                    x_tokens(t, 4)
                    x_tokens(t, 5)
                    decay_matrix(t, 2)
                    c_channels(t, 2)
                    scan_y(t, 2)
                    scan_state(t, 2)


_INS = ["x", "L0_conv_W_in", "L0_conv_W_conv", "L0_conv_b_conv", "L0_conv_dt_bias", "L0_conv_A_log",
        "L0_conv_D_param", "L0_conv_gamma", "L0_conv_beta", "L0_conv_W_out"]


def kernel(**inputs):
    import numpy as _np
    import concourse.bacc as _bacc
    from concourse import mybir as _mybir
    from concourse.bass_utils import run_bass_kernel_spmd as _run

    nc = _bacc.Bacc("TRN2", target_bir_lowering=False, num_devices=1)
    arrays, args = {}, []
    tiles = lambda v: _np.ascontiguousarray(_np.asarray(v).reshape(MT, 128).T)
    laid = {name: _np.asarray(inputs[name]) for name in _INS[:2]}
    laid["W_conv"] = _np.asarray(inputs["L0_conv_W_conv"]).reshape(9, DI + 2 * NS).T
    laid["b_conv_x"] = tiles(inputs["L0_conv_b_conv"][:DI])
    laid["b_conv_bc"] = _np.asarray(inputs["L0_conv_b_conv"])[DI:, None]
    for name in _INS[4:7]:
        laid[name] = _np.asarray(inputs[name])
    laid["gamma"], laid["beta"] = tiles(inputs["L0_conv_gamma"]), tiles(inputs["L0_conv_beta"])
    laid["W_out"] = _np.asarray(inputs["L0_conv_W_out"])
    for name, a in laid.items():
        a = _np.ascontiguousarray(a)
        arrays[f"in_{name}_dram"] = a
        args.append(nc.dram_tensor(f"in_{name}_dram", a.shape, _mybir.dt.from_np(a.dtype), kind="ExternalInput").ap())
    c = constants()
    arrays["in_consts_dram"] = c
    args.append(nc.dram_tensor("in_consts_dram", c.shape, F32, kind="ExternalInput").ap())
    o = nc.dram_tensor("out_0_dram", (B, H, W, C), F32, kind="ExternalOutput").ap()
    build(nc, *args, o)
    r = _run(nc, [arrays], core_ids=[0])
    return r.results[0]["out_0_dram"]
```

```python
from contextlib import ExitStack

import numpy as np
import concourse.bass as bass
from concourse import mybir

F32 = mybir.dt.float32
F32R = mybir.dt.float32r
ALU = mybir.AluOpType
ACT = mybir.ActivationFunctionType
AX = mybir.AxisListType

B, H, W, C = 8, 64, 64, 384
NG = 32
CG = C // NG
DI = 2 * C
NH, HD, NS = 12, 64, 16
PR = B // 2
TOK = B * W
KC = C // 128
MT = DI // 128
GR = NH // 4
BC = MT
B0, C0, DT0 = 0, 32, 64
BCP = C0 + NS
BCW = DT0 + NH
WIN = 2 * DI + BCW
GN_EPS, LN_EPS = 1e-5, 1e-5
SERIES = [1.0 / (2 * k + 1) for k in range(8)]

IDENT, LATER, UPTO, ONES, SAMEIMG, TRI, HEADOF, MHALF, LNEPS = 0, 128, 256, 384, 512, 544, 608, 612, 616
NCONST = 620


def constants():
    k = np.arange(128)[:, None]
    j = np.arange(128)[None, :]
    same = (k // W) == (j // W)
    c = np.zeros((128, NCONST), np.float32)
    c[:, IDENT:IDENT + 128] = k == j
    c[:, LATER:LATER + 128] = same & (k > j)
    c[:, UPTO:UPTO + 128] = same & (k <= j)
    c[:, ONES:ONES + 128] = 1.0
    c[:, SAMEIMG:SAMEIMG + 32] = (k // W) == (np.arange(32)[None, :] // NS)
    c[:, TRI:TRI + 64] = (k % W) <= np.arange(64)[None, :]
    c[:, HEADOF:HEADOF + 2] = (k // 32) % 2 == np.arange(2)[None, :]
    c[:, MHALF:MHALF + 4] = -0.5
    c[:, LNEPS:LNEPS + 4] = LN_EPS
    return c


class Row:

    def __init__(self, i, j):
        self.i, self.j = i, j

    def back(self, lag):
        return Row(self.i, self.j - lag)

    @property
    def parity(self):
        return self.j % 2

    @property
    def static(self):
        return isinstance(self.i, int)

    def last(self):
        return self.static and 2 * self.i + self.j == H - 1

    def exists(self):
        return not self.static or 0 <= 2 * self.i + self.j < H

    def number(self):
        return self.i * 2 + self.j

    def count(self, per_row, k):
        return self.i * (2 * per_row) + (self.j * per_row + k)

    def count_half(self, per_row, k):
        return self.i * per_row + ((self.j // 2) * per_row + k)


PER_ROW = dict(
    z_mm=6, yT_mm=6, xT_mm=3, cv_mm=7, out_mm=4, dtT_mm=1, bcg_mm=1, se_mm=1, xk_mm=6, df_mm=6,
    cet_mm=3, y_mm=3, st_mm=3,
    sz=6, ya=6, xh=3, dtv=1, du=2, de=1, bc_act=2, xc_act=6, xk=6, L=6, cet=3, sbd=3,
    xl=3, tap=63, dch=18, gb=3, yv=6, bst=12, ss=3, agg=4, yn=4, ot=4,
    xn=2, R=6, Mv=6, be=3, ce=3, xd=3, xD=3, sd=3, rs=2, yp=6,
)

FILLS = [
    ("dtT", 0, 0, "dch", 1), ("xk", 0, 1, "xk", 1), ("z", 0, 1, "sz", 1), ("bcg", 0, 1, "gb", 3),
    ("z", 1, 1, "sz", 2), ("df", 1, 1, "L", 2), ("z", 2, 1, "sz", 3), ("yT", 0, 2, "ya", 1),
    ("yT", 1, 2, "ya", 2), ("z", 3, 1, "sz", 4), ("xk", 1, 1, "xk", 2), ("z", 4, 1, "sz", 5),
    ("yT", 2, 2, "ya", 3), ("z", 5, 1, "sz", 6), ("xk", 2, 1, "xk", 3), ("cet", 0, 1, "cet", 1),
    ("yT", 3, 2, "ya", 4), ("yT", 4, 2, "ya", 5), ("xT", 0, -1, "xl", 1), ("yT", 5, 2, "ya", 6),
    ("xk", 3, 1, "xk", 4), ("xT", 1, -1, "xl", 2), ("df", 2, 1, "L", 3), ("xT", 2, -1, "xl", 3),
    ("out", 0, 2, "ot", 1), ("df", 3, 1, "L", 4), ("cet", 1, 1, "cet", 2), ("st", 0, 1, "ss", 1),
    ("out", 1, 2, "ot", 2), ("xk", 4, 1, "xk", 5), ("df", 4, 1, "L", 5), ("out", 2, 2, "ot", 3),
    ("xk", 5, 1, "xk", 6), ("df", 5, 1, "L", 6), ("cet", 2, 1, "cet", 3), ("st", 1, 1, "ss", 2),
    ("out", 3, 2, "ot", 4), ("st", 2, 1, "ss", 3), ("se", 0, 0, "de", 1), ("df", 0, 0, "L", 1),
]
PLACE = {(f[0], f[1]): n for n, f in enumerate(FILLS)}
LAG = {(f[0], f[1]): f[2] for f in FILLS}
assert len(FILLS) % 4 == 0


def build(nc, x, W_in, W_conv, b_conv_x, b_conv_bc, dt_bias, A_log, D_param, gamma, beta, W_out, consts, out):
    with ExitStack() as ctx:
        def sb(name, shape, dt=F32):
            return ctx.enter_context(nc.sbuf_tensor(name, shape, dt))

        def ps(name, shape=(128, 512)):
            return ctx.enter_context(nc.psum_tensor(name, list(shape), F32))

        def semaphore(name):
            return ctx.enter_context(nc.semaphore(name))

        cst = sb("cst", [128, NCONST])
        win_hi = sb("win_hi", [128, KC, WIN], F32R)
        win_lo = sb("win_lo", [128, KC, WIN], F32R)
        wout = sb("wout", [128, MT, C])
        wcv = sb("wcv", [128, MT, 9])
        wcv_bc = sb("wcv_bc", [BCP, 9])
        bcv = sb("bcv", [128, MT])
        bcv_bc = sb("bcv_bc", [BCP, 1])
        gam = sb("gam", [128, MT])
        bet = sb("bet", [128, MT])
        dtb = sb("dtb", [128, NH])
        negA = sb("negA", [128, NH])
        Dp = sb("Dp", [128, NH])
        gn_s = sb("gn_s", [128, PR * NG])
        gn_t = sb("gn_t", [128, PR * NG])
        xt = sb("xt", [128, 2, PR, C])
        xhi = sb("xhi", [128, 2, KC, TOK], F32R)
        xlo = sb("xlo", [128, 2, KC, TOK], F32R)
        acc = sb("acc", [128, 2, MT, TOK])
        acc_bc = sb("acc_bc", [BCP, 2, TOK])
        xc = sb("xc", [128, 2, TOK])
        xc_bc = sb("xc_bc", [BCP, TOK])
        thin = sb("thin", [NS, TOK])
        bcB, bcC, dtv = xc_bc[B0:B0 + NS, :], thin[:, :], thin[0:NH, :]
        sm = sb("sm", [128, 9, PR * NH])
        dt = sb("dt", [128, 2, PR, NH])
        dA = sb("dA", [128, 2, PR, NH])
        dAs = sb("dAs", [128, 2, GR, 2, 2, 8])
        later_r = sb("later_r", [128, 128], F32R)
        DE = sb("DE", [128, 108])
        G = sb("G", [128, PR, W])
        Bbd = sb("Bbd", [128, PR, 2, NS])
        Cbd = sb("Cbd", [128, PR, 2, NS])
        R = sb("R", [128, 2, 8, W], F32R)
        L = sb("L", [128, PR, 4, W])
        BE = sb("BE", [128, PR, 4, 2 * NS])
        CE = sb("CE", [128, PR, 4, 2 * NS])
        CET = sb("CET", [128, PR, 128])
        S = sb("S", [128, GR, PR, HD])
        Sbd = sb("Sbd", [128, PR, 2, HD])
        Xtok = sb("Xtok", [128, 2, PR, 4 * HD])
        Xd = sb("Xd", [128, 2, PR, 4 * HD])
        y = sb("y", [128, PR, DI])
        bst = sb("bst", [128, PR, GR, 6])
        mv = sb("mv", [128, PR, 2])
        vare = sb("vare", [128, PR])
        rstd = sb("rstd", [128, PR])
        ya = sb("ya", [128, 2, TOK])
        yprime = sb("yprime", [128, 2, MT, TOK])
        xres = sb("xres", [128, 2, C])

        shared = [ps(f"shared{n}") for n in range(4)]
        cbank = [ps(f"conv{n}") for n in range(2)]
        ybank = [ps(f"ybank{n}") for n in range(2)]

        ident = cst[:, IDENT:IDENT + 128]
        tri = cst[:, TRI:TRI + W]
        sameimg = cst[:, SAMEIMG:SAMEIMG + 32]

        sem = {name: semaphore(name) for name in PER_ROW}
        s_const = semaphore("s_const")
        s_wst = semaphore("s_wst")
        s_wsplit = semaphore("s_wsplit")
        s_prep = semaphore("s_prep")
        s_init = semaphore("s_init")
        s_chunk = [semaphore("s_chunk0"), semaphore("s_chunk1")]
        s_sqr = semaphore("s_sqr")
        s_red = semaphore("s_red")
        s_var = semaphore("s_var")
        s_sum = semaphore("s_sum")
        s_pow = semaphore("s_pow")
        s_gn = semaphore("s_gn")
        s_last = semaphore("s_last")
        s_xin = [semaphore("s_xin0"), semaphore("s_xin1")]
        s_xr = [semaphore("s_xr0"), semaphore("s_xr1")]
        s_st = [semaphore("s_st0"), semaphore("s_st1")]

        def wait(eng, name, row, k):
            v = row.count(PER_ROW[name], k)
            if isinstance(v, int) and v <= 0:
                return
            eng.wait_ge(sem[name], v)

        def settle(eng):
            eng.nop(nofuse=True)

        def wait_half(eng, s, row, per_row, k):
            v = row.count_half(per_row, k)
            if isinstance(v, int) and v <= 0:
                return
            eng.wait_ge(s, v)

        def wait_free(eng, row, name, n):
            at = PLACE[name, n]
            t = row.back(-LAG[name, n])
            place, back = at - 4, 0
            while back < 4:
                if place < 0:
                    place, back = place + len(FILLS), back + 1
                _, _, lag, reader, k = FILLS[place]
                row = t.back(back + lag)
                if row.exists():
                    wait(eng, reader, row, k)
                    break
                place -= 4
            return shared[at % 4]

        def bank_of(name, n):
            return shared[PLACE[name, n] % 4]

        def conv_bank(t, tile):
            o = 0 if tile == BC else tile + 1
            return cbank[(t.parity + o) % 2]

        def steps(eng):
            def rows(t):
                return t.back(-1), t, t.back(1), t.back(2)

            for t in range(-1, 4):
                yield rows(Row(t // 2, t % 2))
            with eng.Fori(2, H // 2 - 1) as i:
                for j in range(2):
                    yield rows(Row(i, j))
            for t in range(H - 2, H + 2):
                yield rows(Row(t // 2, t % 2))

        NCHUNK, CTOK = 4, 8
        stage = [y[:, :, :].rearrange("p a b -> p (a b)"), yprime[:, 0].rearrange("p a b -> p (a b)")]
        squares = acc[:, 0, :, :].rearrange("p a b -> p (a b)")
        sq_part = sm[:, 0:3, :].rearrange("p a b -> p (a b)")[:, 0:NCHUNK * NG].rearrange("p (c g) -> p c g", g=NG)
        gnw = L[:, :, :, :].rearrange("p a b c -> p (a b c)")
        sq_sum, ex, ex2, var, rs_g = (gnw[:, n * NG:(n + 1) * NG] for n in range(5))
        veps = gnw[:, 5 * NG:6 * NG]
        mhalf32 = gnw[:, 6 * NG:7 * NG]
        s8 = gnw[:, 256:512]
        t8 = gnw[:, 512:768]
        wst = [acc[:, 0, :, :].rearrange("p a b -> p (a b)"), acc[:, 1, :, :].rearrange("p a b -> p (a b)")]

        block = ctx.enter_context(nc.Block())

        @block.sync
        def _(sp):
            sp.dma_start(cst[:, :], consts[:, :]).then_inc(s_const, 16)
            for k in range(2):
                sp.dma_start(wst[k][:, 0:W_in.shape[1]], W_in[128 * k:128 * k + 128, :]).then_inc(s_wst, 16)
            sp.dma_start(wout[:, :, :], W_out.rearrange("(m p) n -> p m n", p=128)).then_inc(s_const, 16)
            sp.dma_start(wcv[:, :, :], W_conv[0:DI, :].rearrange("(m p) k -> p m k", p=128)).then_inc(s_const, 16)
            sp.dma_start(bcv[:, :], b_conv_x[:, :]).then_inc(s_const, 16)
            sp.wait_ge(s_init, 2)
            for at, n in ((B0, DI), (C0, DI + NS)):
                sp.dma_start(wcv_bc[at:at + NS, :], W_conv[n:n + NS, :]).then_inc(s_const, 16)
                sp.dma_start(bcv_bc[at:at + NS, :], b_conv_bc[n - DI:n - DI + NS, :]).then_inc(s_const, 16)
            sp.dma_start(gam[:, :], gamma[:, :]).then_inc(s_const, 16)
            sp.dma_start(bet[:, :], beta[:, :]).then_inc(s_const, 16)
            for dst, v in ((dtb, dt_bias), (negA, A_log), (Dp, D_param)):
                sp.dma_start(dst[:, :], v.rearrange("(a h) -> a h", a=1).to_broadcast([128, NH])).then_inc(s_const, 16)
            sp.wait_ge(s_wsplit, 8)
            sp.dma_start(wst[0][:, 0:W_in.shape[1]], W_in[256:384, :]).then_inc(s_wst, 16)

            xi = x.rearrange("b h w c -> b (h w c)").rearrange("b (p n) -> b p n", p=128)

            def image_chunks(im):
                for c in range(NCHUNK):
                    n = im * NCHUNK + (c - 2)
                    if n >= 0:
                        sp.wait_ge(s_sqr, n + 1)
                        sp.wait_ge(s_sum, im * (NCHUNK + 1) + (c - 1 if c >= 2 else c - 2))
                    src = xi[im, :, c * CTOK * C:(c + 1) * CTOK * C]
                    sp.dma_start(stage[c % 2][:, :], src).then_inc(s_chunk[c % 2], 16)

            for im in range(B):
                image_chunks(im)

            xpair = x.rearrange("(p i) h w c -> i h w p c", i=2)
            opair = out.rearrange("(p i) h w c -> i h w p c", i=2)

            def row_of(v, i, row):
                return v[i][bass.ds(row.number(), 1)].rearrange("a w p c -> w (a p) c")

            def load_row(row):
                for i in range(2):
                    sp.dma_start(xt[64 * i:64 * i + 64, row.parity], row_of(xpair, i, row)).then_inc(s_xin[row.parity], 16)

            def load_residual(row, p):
                v = row.count(64, 32 * (p // 2))
                if not (isinstance(v, int) and v <= 0):
                    sp.wait_ge(s_st[p % 2], v)
                for i in range(2):
                    sp.dma_start(xres[64 * i:64 * i + 64, p % 2], row_of(xpair, i, row)[:, p]).then_inc(s_xr[p % 2], 16)

            load_row(Row(0, 0))
            load_row(Row(0, 1))
            for n, t, r, q in steps(sp):
                if t.exists() and n.back(-1).exists():
                    wait(sp, "xT_mm", t, 3)
                    load_row(n.back(-1))
                if q.exists():
                    for p in range(2):
                        load_residual(q, p)
                    for p in range(PR):
                        wait(sp, "ot", q, p + 1)
                        for i in range(2):
                            sp.dma_start(row_of(opair, i, q)[:, p], xres[64 * i:64 * i + 64, p % 2]).then_inc(s_st[p % 2], 16)
                        if p < 2:
                            load_residual(q, p + 2)
            for s in range(2):
                sp.wait_ge(s_st[s], 64 * H)

        @block.gpsimd
        def _(pool):
            pool.memset(mhalf32, -0.5).then_inc(s_pow, 1)

            def image_pow(im):
                pool.wait_ge(s_red, im * 9 + 8)
                if isinstance(im, int):
                    pool.wait_ge(s_pow, 1)
                pool.tensor_tensor(rs_g, veps, mhalf32, ALU.pow).then_inc(s_pow, 1)

            image_pow(0)
            with pool.Fori(1, B) as im:
                image_pow(im)

            pool.wait_ge(s_const, 16 * 13)
            pool.wait_ge(s_prep, 2)
            pool.wait_ge(s_gn, 4)
            pool.wait_ge(s_init, 13)

            def scale_row(n):
                if not n.exists():
                    return
                v = xt[:, n.parity].rearrange("p a (g c) -> p (a g) c", c=CG)
                wait_half(pool, s_xin[n.parity], n, 32, 32)
                pool.tensor_tensor(v, v, gn_s[:, :].unsqueeze(2).to_broadcast([128, PR * NG, CG]), ALU.mult).then_inc(sem["xn"], 1)

            def shift_row(n):
                if not n.exists():
                    return
                v = xt[:, n.parity].rearrange("p a (g c) -> p (a g) c", c=CG)
                wait(pool, "xn", n, 1)
                pool.tensor_tensor(v, v, gn_t[:, :].unsqueeze(2).to_broadcast([128, PR * NG, CG]), ALU.add).then_inc(sem["xn"], 1)

            def decay_steps(r, m):
                if not r.exists():
                    return
                g, b = m // 2, m % 2
                wait(pool, "dch", r, 18)
                wait(pool, "df_mm", r, m)
                a = dAs[:, r.parity, g, b].rearrange("p s h -> p (s h)").unsqueeze(2).to_broadcast([128, 16, W])
                pool.tensor_tensor(R[:, :, :, :].rearrange("p s h l -> p (s h) l"), a,
                                   tri.unsqueeze(1).to_broadcast([128, 16, W]), ALU.mult).then_inc(sem["R"], 1)

            def scale_BC(r, g, name):
                if not r.exists():
                    return
                wait(pool, "gb", r, 3)
                wait(pool, "de", r, 1)
                dst, src, e, reader = {"be": (BE, Bbd, 0, "st_mm"), "ce": (CE, Cbd, 1, "cet_mm")}[name]
                wait(pool, reader, r, g)
                d = DE[:, 0:96].rearrange("p (e a h) -> p e a h", e=2, a=PR)
                v = src[:, :, :, :].rearrange("p a i n -> p a (i n)").unsqueeze(2).to_broadcast([128, PR, 4, 2 * NS])
                w = d[:, e, :, 4 * g:4 * g + 4].unsqueeze(3).to_broadcast([128, PR, 4, 2 * NS])
                pool.tensor_tensor(dst[:, :, :, :], v, w, ALU.mult).then_inc(sem[name], 1)

            def masked(r, g):
                if not r.exists():
                    return
                for b in range(2):
                    wait(pool, "L", r, 2 * g + b + 1)
                    wait(pool, "gb", r, 1)
                    v = L[:, 2 * b:2 * b + 2]
                    pool.tensor_tensor(v, v, G[:, 2 * b:2 * b + 2].unsqueeze(2).to_broadcast([128, 2, 4, W]),
                                       ALU.mult).then_inc(sem["Mv"], 1)

            def x_dt(r, g):
                if not r.exists():
                    return
                slot = (r.parity + g) % 2
                wait(pool, "dch", r, 15)
                wait(pool, "xk", r, 2 * g + 2)
                wait(pool, "st_mm", r, g - 1)
                wait(pool, "y_mm", r, g - 1)
                w = dt[:, r.parity, :, 4 * g:4 * g + 4].unsqueeze(3).to_broadcast([128, PR, 4, HD])
                pool.tensor_tensor(Xd[:, slot].rearrange("p a (h d) -> p a h d", h=4),
                                   Xtok[:, slot].rearrange("p a (h d) -> p a h d", h=4), w, ALU.mult).then_inc(sem["xd"], 1)

            def x_D(r, g):
                if not r.exists():
                    return
                xv = Xtok[:, (r.parity + g) % 2].rearrange("p a (h d) -> p a h d", h=4)
                wait(pool, "xd", r, g + 1)
                w = Dp[:, 4 * g:4 * g + 4].unsqueeze(1).unsqueeze(3).to_broadcast([128, PR, 4, HD])
                pool.tensor_tensor(xv, xv, w, ALU.mult).then_inc(sem["xD"], 1)

            def decay_state(r, g):
                if not r.exists():
                    return
                wait(pool, "sbd", r, g + 1)
                wait(pool, "de", r, 1)
                dec = DE[:, 96:108].rearrange("p (a g) -> p a g", a=PR)[:, :, g].unsqueeze(2).to_broadcast([128, PR, HD])
                pool.tensor_tensor(S[:, g], S[:, g], dec, ALU.mult).then_inc(sem["sd"], 1)

            def ln_scale(q):
                if not q.exists():
                    return
                wait(pool, "agg", q, 4)
                pool.tensor_tensor(vare[:, :], mv[:, :, 1], cst[:, LNEPS:LNEPS + PR], ALU.add).then_inc(sem["rs"], 1)
                wait(pool, "rs", q, 1)
                pool.tensor_tensor(rstd[:, :], vare[:, :], cst[:, MHALF:MHALF + PR], ALU.pow).then_inc(sem["rs"], 1)

            def gated(q, m):
                if not q.exists():
                    return
                wait(pool, "ya", q, m + 1)
                wait(pool, "sz", q, m + 1)
                v = yprime[:, q.parity, m]
                pool.tensor_tensor(v, ya[:, m % 2], v, ALU.mult).then_inc(sem["yp"], 1)

            for n, t, r, q in steps(pool):
                x_D(q, 2)
                scale_row(n)
                decay_steps(r, 1)
                shift_row(n)
                ln_scale(q)
                masked(r, 0)
                decay_steps(r, 2)
                gated(q, 0)
                scale_BC(r, 0, "ce")
                gated(q, 1)
                x_dt(r, 0)
                gated(q, 2)
                decay_state(r, 0)
                scale_BC(r, 0, "be")
                scale_BC(r, 1, "ce")
                for m in range(3, 5):
                    gated(q, m)
                x_D(r, 0)
                gated(q, 5)
                x_dt(r, 1)
                decay_steps(r, 3)
                decay_state(r, 1)
                masked(r, 1)
                scale_BC(r, 1, "be")
                scale_BC(r, 2, "ce")
                decay_steps(r, 4)
                x_D(r, 1)
                decay_steps(r, 5)
                x_dt(r, 2)
                scale_BC(r, 2, "be")
                decay_steps(t, 0)
                decay_state(r, 2)
                masked(r, 2)

        @block.scalar
        def _(act):
            act.wait_ge(s_const, 16 * 13)
            act.activation(negA[:, :], negA[:, :], ACT.Exp).then_inc(s_prep, 1)
            act.wait_ge(s_prep, 1)
            act.mul(negA[:, :], negA[:, :], -1.0).then_inc(s_prep, 1)
            act.wait_ge(s_wsplit, 3 * 8)

            def image_squares(im):
                for c in range(NCHUNK):
                    act.wait_ge(s_chunk[c % 2], (im * (NCHUNK // 2) + (c // 2 + 1)) * 16)
                    if not (isinstance(im, int) and im == 0 and c == 0):
                        act.wait_ge(s_red, im * 9 + (c if c else -4))
                    act.activation(squares, stage[c % 2], ACT.Square).then_inc(s_sqr, 1)

            image_squares(0)
            with act.Fori(1, B) as im:
                image_squares(im)

            def gate(r, m):
                if not r.exists():
                    return
                wait(act, "z_mm", r, m + 1)
                wait(act, "out_mm", r.back(1), 0)
                act.activation(yprime[:, r.parity, m], bank_of("z", m)[:, :], ACT.Silu).then_inc(sem["sz"], 1)

            def affine(q, m):
                if not q.exists():
                    return
                wait(act, "yT_mm", q, m + 1)
                wait(act, "yp", q, m - 1)
                act.activation(ya[:, m % 2], bank_of("yT", m)[:, :], ACT.Identity, bias=bet[:, m:m + 1],
                               scale=gam[:, m:m + 1]).then_inc(sem["ya"], 1)

            def x_hi(n, k):
                if not n.exists():
                    return
                wait(act, "xT_mm", n, k + 1)
                wait(act, "z_mm", n.back(2), 6)
                wait(act, "cv_mm", n.back(2), 7)
                act.activation(xhi[:, n.parity, k], bank_of("xT", k)[:, :], ACT.Copy).then_inc(sem["xh"], 1)

            def take_dt(t):
                if not t.exists():
                    return
                wait(act, "cv_mm", t, 1)
                wait(act, "bcg_mm", t.back(1), 0)
                act.activation(dtv, conv_bank(t, BC)[DT0:DT0 + NH, :], ACT.Copy).then_inc(sem["dtv"], 1)

            def silu_bc(r):
                if not r.exists():
                    return
                if r.last():
                    act.wait_ge(s_last, 1)
                else:
                    wait(act, "tap", r.back(-1), 5)
                    wait(act, "dtT_mm", r.back(-1), 1)
                wait(act, "bcg_mm", r, 0)
                act.activation(bcB, bcB, ACT.Silu).then_inc(sem["bc_act"], 1)
                act.activation(bcC, xc_bc[C0:C0 + NS, :], ACT.Silu).then_inc(sem["bc_act"], 1)

            def decays(r):
                if not r.exists():
                    return
                wait(act, "se_mm", r, 1)
                wait(act, "be", r, 0)
                wait(act, "ce", r, 0)
                wait(act, "sd", r, 0)
                act.activation(DE[:, :], bank_of("se", 0)[:, 0:108], ACT.Exp).then_inc(sem["de"], 1)

            def silu_conv(r, j):
                if not r.exists():
                    return
                if r.last():
                    act.wait_ge(s_last, j + 2)
                else:
                    wait(act, "tap", r.back(-1), 9 * (j + 1) + 5)
                act.activation(xc[:, j % 2], xc[:, j % 2], ACT.Silu).then_inc(sem["xc_act"], 1)

            def take_x(r, j):
                if not r.exists():
                    return
                g = j // 2
                wait(act, "xk_mm", r, j + 1)
                wait(act, "yv", r, 2 * g - 2)
                wait(act, "xd", r, g - 1)
                src = bank_of("xk", j)[:, :].rearrange("p (a c) -> p a c", a=PR)
                act.activation(Xtok[:, (r.parity + g) % 2, :, 128 * (j % 2):128 * (j % 2) + 128], src,
                               ACT.Copy).then_inc(sem["xk"], 1)

            def state_blocks(r, g):
                if not r.exists():
                    return
                wait(act, "ss", r.back(1), g + 1)
                wait(act, "y_mm", r, g)
                for h in range(2):
                    last = act.activation(Sbd[:, :, h], S[:, g], ACT.Copy, scale=cst[:, HEADOF + h:HEADOF + h + 1])
                last.then_inc(sem["sbd"], 1)

            def exp_decay(r, m):
                if not r.exists():
                    return
                b = m % 2
                wait(act, "df_mm", r, m + 1)
                wait(act, "y_mm", r, m // 2)
                src = bank_of("df", m)[:, :].rearrange("p (a h l) -> p a h l", a=2, h=4)
                act.activation(L[:, 2 * b:2 * b + 2], src, ACT.Exp).then_inc(sem["L"], 1)

            def take_cet(r, g):
                if not r.exists():
                    return
                wait(act, "cet_mm", r, g + 1)
                wait(act, "y_mm", r, g)
                act.activation(CET[:, :, :], bank_of("cet", g)[:, :].rearrange("p (a l) -> p a l", a=PR),
                               ACT.Copy).then_inc(sem["cet"], 1)

            def softplus_exp(t):
                if not t.exists():
                    return
                wait(act, "dch", t, 1)
                act.activation(sm[:, 1], sm[:, 0], ACT.Abs).then_inc(sem["du"], 1)
                wait(act, "du", t, 1)
                act.activation(sm[:, 2], sm[:, 1], ACT.Exp, scale=-1.0).then_inc(sem["du"], 1)

            act.wait_ge(s_init, 13)
            for n, t, r, q in steps(act):
                x_hi(t, 2)
                for m in range(2, 4):
                    exp_decay(q, m)
                take_cet(q, 1)
                take_dt(t)
                silu_conv(q, 5)
                exp_decay(q, 4)
                for m in range(4, 6):
                    take_x(q, m)
                exp_decay(q, 5)
                take_cet(q, 2)
                state_blocks(q, 2)
                decays(r)
                silu_bc(r)
                silu_conv(r, 0)
                exp_decay(r, 0)
                gate(r, 0)
                take_x(r, 0)
                softplus_exp(t)
                exp_decay(r, 1)
                gate(r, 1)
                state_blocks(r, 0)
                silu_conv(r, 1)
                gate(r, 2)
                for m in range(0, 2):
                    affine(q, m)
                gate(r, 3)
                silu_conv(r, 2)
                take_x(r, 1)
                gate(r, 4)
                affine(q, 2)
                gate(r, 5)
                take_x(r, 2)
                take_cet(r, 0)
                for m in range(3, 6):
                    affine(q, m)
                silu_conv(r, 3)
                x_hi(n, 0)
                take_x(r, 3)
                state_blocks(r, 1)
                x_hi(n, 1)
                silu_conv(r, 4)

        @block.vector
        def _(dve):
            dve.memset(wcv_bc[:, :], 0.0).then_inc(s_init, 1)
            dve.memset(bcv_bc[:, :], 0.0).then_inc(s_init, 1)
            for w in (win_hi, win_lo):
                dve.memset(w[:, :, 2 * DI:WIN].bitcast(F32), 0.0).then_inc(s_init, 1)
            dve.memset(S[:, :, :, :], 0.0).then_inc(s_init, 1)
            dve.wait_ge(s_init, 5)
            spans = [(0, 2 * DI, 0), (2 * DI, 2 * DI + NS, 2 * DI + B0), (2 * DI + NS, 2 * DI + 2 * NS, 2 * DI + C0),
                     (2 * DI + 2 * NS, 2 * DI + 2 * NS + NH, 2 * DI + DT0)]
            for k, slot in ((0, 0), (1, 1), (2, 0)):
                dve.wait_ge(s_wst, 48 if k == 2 else 32)
                for n, (a, b, at) in enumerate(spans):
                    dve.tensor_copy(win_hi[:, k, at:at + b - a], wst[slot][:, a:b]).then_inc(s_wsplit, 1)
                dve.wait_ge(s_wsplit, 8 * k + 4)
                for n, (a, b, at) in enumerate(spans):
                    dve.tensor_tensor(win_lo[:, k, at:at + b - a], wst[slot][:, a:b],
                                      win_hi[:, k, at:at + b - a].bitcast(F32), ALU.subtract).then_inc(s_wsplit, 1)

            dve.wait_ge(s_const, 16 * 13)
            dve.tensor_copy(later_r[:, :], cst[:, LATER:LATER + 128]).then_inc(s_init, 1)

            def image_stats(im):
                for c in range(NCHUNK):
                    dve.wait_ge(s_sqr, im * NCHUNK + (c + 1))
                    if c == 0 and not isinstance(im, int):
                        dve.wait_ge(s_sum, im * (NCHUNK + 1))
                    dve.tensor_reduce(sq_part[:, c], squares.rearrange("p (n g c) -> p g n c", g=NG, c=CG), AX.XY,
                                      ALU.add).then_inc(s_red, 1)
                dve.wait_ge(s_red, im * 9 + 4)
                dve.tensor_reduce(sq_sum, sq_part.rearrange("p c g -> p g c"), AX.X, ALU.add).then_inc(s_red, 1)
                dve.wait_ge(s_sum, im * (NCHUNK + 1) + (NCHUNK + 1))
                dve.tensor_reduce(ex, cbank[0][:, 0:C].rearrange("p (g c) -> p g c", c=CG), AX.X, ALU.add).then_inc(s_red, 1)
                dve.tensor_scalar(ex2, cbank[1][:, 0:NG], 1.0 / (H * W * CG), GN_EPS, ALU.mult, ALU.add).then_inc(s_red, 1)
                dve.wait_ge(s_red, im * 9 + 7)
                dve.scalar_tensor_tensor(out=var, in0=ex, scalar=-1.0 / (H * W * CG) ** 2, in1=ex, op0=ALU.mult,
                                         op1=ALU.mult).then_inc(s_var, 1)
                dve.wait_ge(s_var, im * 3 + 1)
                dve.tensor_tensor(veps, ex2, var, ALU.add).then_inc(s_red, 1)
                dve.wait_ge(s_pow, im + 2)
                dve.tensor_copy(s8[:, bass.ts(im, NG)], rs_g).then_inc(s_var, 1)
                dve.scalar_tensor_tensor(out=t8[:, bass.ts(im, NG)], in0=ex, scalar=-1.0 / (H * W * CG), in1=rs_g,
                                         op0=ALU.mult, op1=ALU.mult).then_inc(s_var, 1)
                dve.wait_ge(s_var, im * 3 + 3)
                dve.tensor_copy(ex2[:, 0:1], ex2[:, 0:1]).then_inc(s_red, 1)

            image_stats(0)
            with dve.Fori(1, B) as im:
                image_stats(im)
            dve.wait_ge(s_var, 3 * B)
            for dst, src in ((gn_s, s8), (gn_t, t8)):
                v = src.rearrange("p (a i g) -> p a i g", i=2, g=NG)
                for i in range(2):
                    dve.tensor_copy(dst[64 * i:64 * i + 64, :].rearrange("p (a g) -> p a g", g=NG),
                                    v[64 * i:64 * i + 64, :, i]).then_inc(s_gn, 1)

            dve.memset(acc[:, 1], 0.0).then_inc(s_init, 1)
            dve.memset(acc_bc[:, 1], 0.0).then_inc(s_init, 1)
            dve.wait_ge(s_init, 8)
            for m in range(MT):
                ins = dve.tensor_scalar(acc[:, 0, m], acc[:, 1, m], bcv[:, m:m + 1], None, ALU.add)
                if m < MT - 2:
                    ins.then_inc(s_init, 1)
            dve.tensor_scalar(acc_bc[:, 0], acc_bc[:, 1], bcv_bc[:, 0:1], None, ALU.add).then_inc(s_init, 1)
            dve.wait_ge(s_init, 13)

            def taps(t, tile, part, between=None):
                o = 0 if tile == BC else tile + 1
                bank = conv_bank(t, tile)
                if tile == BC:
                    src, done, this, w, bias = bank[0:BCP, :], acc_bc[:, (t.parity + 1) % 2], acc_bc[:, t.parity], wcv_bc, bcv_bc[:, 0:1]
                    dst, tap = xc_bc[:, :], lambda ky, kx: w[:, 3 * ky + kx:3 * ky + kx + 1]
                else:
                    src, done, this, w, bias = bank[:, :], acc[:, (t.parity + 1) % 2, tile], acc[:, t.parity, tile], wcv, bcv[:, tile:tile + 1]
                    dst, tap = xc[:, tile % 2], lambda ky, kx: w[:, tile, 3 * ky + kx:3 * ky + kx + 1]
                s3, d3, a3 = (v.rearrange("p (b w) -> p b w", w=W) for v in (src, done, this))
                begun = d3

                def left(a, ky):
                    return dve.scalar_tensor_tensor(out=a[:, :, 1:W], in0=s3[:, :, 0:W - 1], scalar=tap(ky, 0),
                                                    in1=a[:, :, 1:W], op0=ALU.mult, op1=ALU.add)

                def right(a, ky):
                    return dve.scalar_tensor_tensor(out=a[:, :, 0:W - 1], in0=s3[:, :, 1:W], scalar=tap(ky, 2),
                                                    in1=a[:, :, 0:W - 1], op0=ALU.mult, op1=ALU.add)

                def fill(n):
                    if between is not None:
                        between(n)

                if part == 0:
                    wait(dve, "cv_mm", t, o + 1)
                    wait(dve, "tap", t.back(1), 9 * o + 9)
                    left(d3, 2).then_inc(sem["tap"], 1)
                    fill(0)
                    left(a3, 1).then_inc(sem["tap"], 1)
                    fill(1)
                    wait(dve, "tap", t, 9 * o + 1)
                    right(d3, 2).then_inc(sem["tap"], 1)
                    fill(2)
                    wait(dve, "tap", t, 9 * o + 2)
                    right(a3, 1).then_inc(sem["tap"], 1)
                    fill(3)
                    if tile == BC:
                        wait(dve, "bcg_mm", t.back(1), 0)
                    else:
                        wait(dve, "xk_mm", t.back(1), tile - 1)
                    wait(dve, "tap", t, 9 * o + 3)
                    dve.scalar_tensor_tensor(out=dst, in0=src, scalar=tap(2, 1), in1=done, op0=ALU.mult,
                                             op1=ALU.add).then_inc(sem["tap"], 1)
                    fill(4)
                else:
                    wait(dve, "tap", t, 9 * o + 4)
                    dve.scalar_tensor_tensor(out=this, in0=src, scalar=tap(1, 1), in1=this, op0=ALU.mult,
                                             op1=ALU.add).then_inc(sem["tap"], 1)
                    fill(5)
                    wait(dve, "tap", t, 9 * o + 5)
                    dve.tensor_scalar(done, src, tap(0, 1), bias, ALU.mult, ALU.add).then_inc(sem["tap"], 1)
                    fill(6)
                    wait(dve, "tap", t, 9 * o + 7)
                    left(begun, 0).then_inc(sem["tap"], 1)
                    fill(7)
                    wait(dve, "tap", t, 9 * o + 8)
                    right(begun, 0).then_inc(sem["tap"], 1)
                    fill(8)

            def last_row(r, tile):
                wait(dve, "tap", r, 63)
                if tile == BC:
                    wait(dve, "bcg_mm", r, 0)
                    dve.tensor_copy(xc_bc[:, :], acc_bc[:, r.parity]).then_inc(s_last, 1)
                else:
                    wait(dve, "xk_mm", r, tile - 1)
                    dve.tensor_copy(xc[:, tile % 2], acc[:, r.parity, tile]).then_inc(s_last, 1)

            def softplus_step(t, n):
                v, u, w2, rw, q, s, p, lp, vr = (sm[:, n_] for n_ in (0, 2, 3, 4, 5, 6, 7, 8, 1))
                d = dt[:, t.parity].rearrange("p a h -> p (a h)")

                def done(ins):
                    ins.then_inc(sem["dch"], 1)

                if n == 1:
                    wait(dve, "du", t, 2)
                else:
                    wait(dve, "dch", t, n)
                if n == 1:
                    done(dve.tensor_scalar(w2, u, 2.0, None, ALU.add))
                elif n == 2:
                    done(dve.reciprocal(rw, w2))
                elif n == 3:
                    done(dve.tensor_tensor(q, u, rw, ALU.mult))
                elif n == 4:
                    done(dve.tensor_tensor(s, q, q, ALU.mult))
                elif n == 5:
                    done(dve.tensor_scalar(p, s, SERIES[7], None, ALU.mult))
                elif n <= 11:
                    done(dve.scalar_tensor_tensor(out=p, in0=p, scalar=SERIES[12 - n], in1=s, op0=ALU.add, op1=ALU.mult))
                elif n == 12:
                    done(dve.scalar_tensor_tensor(out=lp, in0=p, scalar=1.0, in1=q, op0=ALU.add, op1=ALU.mult))
                elif n == 13:
                    done(dve.tensor_scalar(vr, v, 0.0, None, ALU.max))
                elif n == 14:
                    wait(dve, "xd", t.back(1), 0)
                    wait(dve, "se_mm", t.back(1), 0)
                    done(dve.scalar_tensor_tensor(out=d, in0=lp, scalar=2.0, in1=vr, op0=ALU.mult, op1=ALU.add))
                elif n == 15:
                    done(dve.tensor_tensor(dA[:, t.parity], dt[:, t.parity],
                                           negA[:, :].unsqueeze(1).to_broadcast([128, PR, NH]), ALU.mult))
                else:
                    wait(dve, "R", t.back(1), 0)
                    for g in range(GR):
                        a = dA[:, t.parity].rearrange("p (b a) (g h) -> p g b a h", b=2, h=4)[:, g]
                        hi, lo = (dAs[:, t.parity, g, :, s_].rearrange("p b (a h) -> p b a h", h=4) for s_ in range(2))
                        if n == 16:
                            ins = dve.tensor_copy(hi.bitcast(F32R), a)
                        else:
                            ins = dve.tensor_tensor(lo, a, hi, ALU.subtract)
                    done(ins)

            def conv_part(t, tile, part):
                if t.exists():
                    between = {4: lambda n: softplus_step(t, n) if n else None,
                               5: lambda n: softplus_step(t, n + 9)}.get(tile)
                    taps(t, tile, part, between)
                elif part == 0 and t.back(1).exists():
                    last_row(t.back(1), tile)

            def add_bias(t):
                if not t.exists():
                    return
                wait(dve, "dtT_mm", t, 1)
                dve.tensor_tensor(sm[:, 0].rearrange("p (a h) -> p a h", a=PR),
                                  bank_of("dtT", 0)[:, 0:PR * NH].rearrange("p (a h) -> p a h", a=PR),
                                  dtb[:, :].unsqueeze(1).to_broadcast([128, PR, NH]), ALU.add).then_inc(sem["dch"], 1)

            def residual(q, p):
                if not q.exists():
                    return
                wait(dve, "out_mm", q, p + 1)
                dve.wait_ge(s_xr[p % 2], q.count(64, 32 * (p // 2) + 32))
                dve.tensor_tensor(xres[:, p % 2], bank_of("out", p)[:, 0:C], xres[:, p % 2], ALU.add).then_inc(sem["ot"], 1)

            def take_y(r, g):
                if not r.exists():
                    return
                slot = (r.parity + g) % 2
                wait(dve, "y_mm", r, g + 1)
                wait(dve, "xD", r, g + 1)
                wait(dve, "yT_mm", r.back(1), 2 * g + 2)
                for b in range(2):
                    at = 256 * g + 128 * b
                    dve.tensor_tensor(y[:, :, at:at + 128], ybank[b][:, :].rearrange("p (a c) -> p a c", a=PR),
                                      Xtok[:, slot, :, 128 * b:128 * b + 128], ALU.add).then_inc(sem["yv"], 1)
                wait(dve, "yv", r, 2 * g + 2)
                for p in range(PR):
                    dve.bn_stats(bst[:, p, g], y[:, p, 256 * g:256 * g + 256]).then_inc(sem["bst"], 1)

            def new_state(r, g):
                if not r.exists():
                    return
                wait(dve, "st_mm", r, g + 1)
                wait(dve, "sd", r, g + 1)
                dve.tensor_tensor(S[:, g], bank_of("st", g)[:, 0:256].rearrange("p (a d) -> p a d", a=PR), S[:, g],
                                  ALU.add).then_inc(sem["ss"], 1)

            def ln_statistics(q):
                if not q.exists():
                    return
                wait(dve, "bst", q, 12)
                settle(dve)
                for p in range(PR):
                    dve.bn_aggr(mv[:, p], bst[:, p].rearrange("p g s -> p (g s)")).then_inc(sem["agg"], 1)

            def ln_normalise(q):
                if not q.exists():
                    return
                wait(dve, "rs", q, 2)
                for p in range(PR):
                    dve.tensor_scalar(y[:, p], y[:, p], mv[:, p, 0:1], rstd[:, p:p + 1], ALU.subtract,
                                      ALU.mult).then_inc(sem["yn"], 1)

            def x_low(n, k):
                if not n.exists():
                    return
                wait(dve, "xh", n, k + 1)
                dve.tensor_tensor(xlo[:, n.parity, k], bank_of("xT", k)[:, :], xhi[:, n.parity, k].bitcast(F32),
                                  ALU.subtract).then_inc(sem["xl"], 1)

            def b_and_c_tokens(r):
                if not r.exists():
                    return
                wait(dve, "bcg_mm", r, 1)
                wait(dve, "Mv", r, 0)
                wait(dve, "be", r, 0)
                wait(dve, "ce", r, 0)
                bank = bank_of("bcg", 0)
                dve.tensor_tensor(G[:, :, :], bank[:, 0:256].rearrange("p (a l) -> p a l", a=PR),
                                  tri.unsqueeze(1).to_broadcast([128, PR, W]), ALU.mult).then_inc(sem["gb"], 1)
                for m, dst in enumerate((Bbd, Cbd)):
                    v = bank[:, 256 + 64 * m:320 + 64 * m].rearrange("p (a n) -> p a n", a=PR).unsqueeze(2)
                    dve.tensor_tensor(dst[:, :, :, :], v.to_broadcast([128, PR, 2, NS]),
                                      sameimg.rearrange("p (i n) -> p i n", i=2).unsqueeze(1).to_broadcast([128, PR, 2, NS]),
                                      ALU.mult).then_inc(sem["gb"], 1)

            for n, t, r, q in steps(dve):
                ln_normalise(q)
                conv_part(t, 2, 0)
                conv_part(t, 2, 1)
                conv_part(t, 3, 0)
                conv_part(t, 3, 1)
                conv_part(t, 4, 0)
                x_low(n, 0)
                conv_part(t, 4, 1)
                for m in range(1, 3):
                    x_low(n, m)
                take_y(r, 0)
                residual(q, 0)
                conv_part(t, 5, 0)
                conv_part(t, 5, 1)
                residual(q, 1)
                new_state(r, 0)
                conv_part(n, BC, 0)
                conv_part(n, BC, 1)
                residual(q, 2)
                take_y(r, 1)
                new_state(r, 1)
                conv_part(n, 0, 0)
                residual(q, 3)
                conv_part(n, 0, 1)
                new_state(r, 2)
                add_bias(n)
                conv_part(n, 1, 0)
                take_y(r, 2)
                ln_statistics(r)
                conv_part(n, 1, 1)
                b_and_c_tokens(t)

        @block.tensor
        def _(pe):
            pe.wait_ge(s_const, 16 * 13)

            def image_sums(im):
                for c in range(NCHUNK):
                    pe.wait_ge(s_chunk[c % 2], (im * (NCHUNK // 2) + (c // 2 + 1)) * 16)
                    if c == 0 and not isinstance(im, int):
                        pe.wait_ge(s_red, im * 9)
                    for n in range(CTOK):
                        last = pe.matmul(cbank[0][:, 0:C], cst[:, ONES:ONES + 128], stage[c % 2][:, n * C:(n + 1) * C],
                                         start=(c == 0 and n == 0), stop=(c == NCHUNK - 1 and n == CTOK - 1))
                    last.then_inc(s_sum, 1)
                pe.wait_ge(s_red, im * 9 + 5)
                pe.matmul(cbank[1][:, 0:NG], cst[:, ONES:ONES + 128], sq_sum, start=True, stop=True).then_inc(s_sum, 1)

            image_sums(0)
            with pe.Fori(1, B) as im:
                image_sums(im)

            pe.wait_ge(s_wsplit, 24)
            pe.wait_ge(s_init, 13)

            def project(dst, col, par, width=128):
                n = 0
                for wt, xv in ((win_lo, xhi), (win_hi, xlo), (win_hi, xhi)):
                    for k in range(KC):
                        last = pe.matmul(dst, wt[:, k, col:col + width], xv[:, par, k], start=(n == 0), stop=(n == 3 * KC - 1))
                        n += 1
                return last

            def z_tile(r, m):
                if not r.exists():
                    return
                bank = wait_free(pe, r, "z", m)
                wait(pe, "xl", r, 3)
                project(bank[:, :], 128 * m, r.parity).then_inc(sem["z_mm"], 1)

            def y_transposed(q, m):
                if not q.exists():
                    return
                bank = wait_free(pe, q, "yT", m)
                wait(pe, "yn", q, 4)
                for p in range(PR):
                    last = pe.transpose(bank[:, 128 * p:128 * p + 128], y[:, p, 128 * m:128 * m + 128], ident)
                last.then_inc(sem["yT_mm"], 1)

            def x_transposed(n, k):
                if not n.exists():
                    return
                bank = wait_free(pe, n, "xT", k)
                wait(pe, "xn", n, 2)
                for p in range(PR):
                    last = pe.transpose(bank[:, 128 * p:128 * p + 128], xt[:, n.parity, p, 128 * k:128 * k + 128], ident)
                last.then_inc(sem["xT_mm"], 1)

            def conv_input(t, tile):
                if not t.exists():
                    return
                o = 0 if tile == BC else tile + 1
                wait(pe, "tap", t, 9 * (o - 1))
                wait(pe, "xl", t, 3)
                if o in (1, 2):
                    wait(pe, "dtv", t, o - 1)
                if tile == BC:
                    last = project(conv_bank(t, tile)[0:BCW, :], 2 * DI, t.parity, BCW)
                else:
                    last = project(conv_bank(t, tile)[:, :], DI + 128 * tile, t.parity)
                last.then_inc(sem["cv_mm"], 1)

            def out_pair(q, p):
                if not q.exists():
                    return
                bank = wait_free(pe, q, "out", p)
                wait(pe, "yp", q, 6)
                for m in range(MT):
                    last = pe.matmul(bank[:, 0:C], yprime[:, q.parity, m, 128 * p:128 * p + 128], wout[:, m, :],
                                     start=(m == 0), stop=(m == MT - 1))
                last.then_inc(sem["out_mm"], 1)

            def decay_sums(r):
                if not r.exists():
                    return
                bank = wait_free(pe, r, "se", 0)
                wait(pe, "dch", r, 16)
                a = dA[:, r.parity].rearrange("p a h -> p (a h)")
                pe.matmul(bank[:, 0:48], cst[:, LATER:LATER + 128], a, start=True, stop=True)
                pe.matmul(bank[:, 48:96], cst[:, UPTO:UPTO + 128], a, start=True, stop=True)
                for h in range(4):
                    rhs = dA[:, r.parity].rearrange("p a (g h) -> p a g h", h=4)[:, :, :, h]
                    last = pe.matmul(bank[32 * h:32 * h + 32, 96:108].rearrange("p (a g) -> p a g", a=PR), sameimg, rhs,
                                     start=True, stop=True)
                last.then_inc(sem["se_mm"], 1)

            def b_and_c(r):
                if not r.exists():
                    return
                bank = wait_free(pe, r, "bcg", 0)
                wait(pe, "bc_act", r, 2)
                settle(pe)
                for p in range(PR):
                    for i in range(2):
                        tok = slice(128 * p + 64 * i, 128 * p + 64 * i + 64)
                        pe.matmul(bank[64 * i:64 * i + 64, 64 * p:64 * p + 64], bcB[:, tok], bcC[:, tok], start=True, stop=True)
                for m, v in enumerate((bcB, bcC)):
                    for p in range(PR):
                        at = 256 + 64 * m + 16 * p
                        last = pe.transpose(bank[:, at:at + NS], v[:, 128 * p:128 * p + 128], cst[0:NS, IDENT:IDENT + NS])
                last.then_inc(sem["bcg_mm"], 1)

            def x_tokens(r, j):
                if not r.exists():
                    return
                bank = wait_free(pe, r, "xk", j)
                wait(pe, "xc_act", r, j + 1)
                for p in range(PR):
                    last = pe.transpose(bank[:, 128 * p:128 * p + 128], xc[:, j % 2, 128 * p:128 * p + 128], ident)
                last.then_inc(sem["xk_mm"], 1)

            def decay_matrix(r, m):
                if not r.exists():
                    return
                bank = wait_free(pe, r, "df", m)
                wait(pe, "R", r, m + 1)
                for part in range(2):
                    last = pe.matmul(bank[:, :], later_r[:, :], R[:, part].rearrange("p h l -> p (h l)"),
                                     start=(part == 0), stop=(part == 1))
                last.then_inc(sem["df_mm"], 1)

            def c_channels(r, g):
                if not r.exists():
                    return
                bank = wait_free(pe, r, "cet", g)
                wait(pe, "ce", r, g + 1)
                for p in range(PR):
                    last = pe.transpose(bank[:, 128 * p:128 * p + 128], CE[:, p].rearrange("p h n -> p (h n)"), ident)
                last.then_inc(sem["cet_mm"], 1)

            def scan_y(r, g):
                if not r.exists():
                    return
                slot = (r.parity + g) % 2
                wait(pe, "yv", r, 2 * g)
                wait(pe, "cet", r, g + 1)
                wait(pe, "sbd", r, g + 1)
                for p in range(PR):
                    for b in range(2):
                        rows = slice(64 * b, 64 * b + 64)
                        pe.matmul(ybank[b][:, 128 * p:128 * p + 128], CET[rows, p], Sbd[rows, p].rearrange("p h d -> p (h d)"),
                                  start=(p == 0), stop=False, skip_group_check=True)
                wait(pe, "Mv", r, 2 * g + 2)
                wait(pe, "xd", r, g + 1)
                settle(pe)
                for p in range(PR):
                    for hh in range(2):
                        for i, b in ((0, 0), (1, 1), (0, 1), (1, 0)):
                            h = 2 * b + hh
                            part = slice(64 * i, 64 * i + 64)
                            at = 128 * p + 64 * hh
                            last = pe.matmul(ybank[b][part, at:at + 64], L[part, p, h], Xd[part, slot, p, 64 * h:64 * h + 64],
                                             start=False, stop=True, skip_group_check=True)
                last.then_inc(sem["y_mm"], 1)

            def scan_state(r, g):
                if not r.exists():
                    return
                slot = (r.parity + g) % 2
                bank = wait_free(pe, r, "st", g)
                wait(pe, "be", r, g + 1)
                wait(pe, "xd", r, g + 1)
                for p in range(PR):
                    for h in range(4):
                        last = pe.matmul(bank[32 * h:32 * h + 32, 64 * p:64 * p + 64], BE[:, p, h],
                                         Xd[:, slot, p, 64 * h:64 * h + 64], start=True, stop=True)
                last.then_inc(sem["st_mm"], 1)

            def dt_tokens(t):
                if not t.exists():
                    return
                bank = wait_free(pe, t, "dtT", 0)
                wait(pe, "dtv", t, 1)
                settle(pe)
                for p in range(PR):
                    last = pe.transpose(bank[:, NH * p:NH * p + NH], dtv[:, 128 * p:128 * p + 128], cst[0:NH, IDENT:IDENT + NH])
                last.then_inc(sem["dtT_mm"], 1)

            for n, t, r, q in steps(pe):
                conv_input(t, 1)
                dt_tokens(t)
                scan_y(q, 2)
                x_tokens(r, 0)
                conv_input(t, 2)
                z_tile(r, 0)
                b_and_c(r)
                z_tile(r, 1)
                decay_matrix(r, 1)
                z_tile(r, 2)
                conv_input(t, 3)
                for m in range(0, 2):
                    y_transposed(q, m)
                z_tile(r, 3)
                x_tokens(r, 1)
                z_tile(r, 4)
                y_transposed(q, 2)
                z_tile(r, 5)
                x_tokens(r, 2)
                c_channels(r, 0)
                y_transposed(q, 3)
                conv_input(t, 4)
                y_transposed(q, 4)
                x_transposed(n, 0)
                y_transposed(q, 5)
                scan_y(r, 0)
                x_tokens(r, 3)
                conv_input(t, 5)
                x_transposed(n, 1)
                decay_matrix(r, 2)
                x_transposed(n, 2)
                out_pair(q, 0)
                decay_matrix(r, 3)
                conv_input(n, BC)
                c_channels(r, 1)
                scan_state(r, 0)
                out_pair(q, 1)
                scan_y(r, 1)
                x_tokens(r, 4)
                decay_matrix(r, 4)
                out_pair(q, 2)
                x_tokens(r, 5)
                decay_matrix(r, 5)
                conv_input(n, 0)
                c_channels(r, 2)
                scan_state(r, 1)
                out_pair(q, 3)
                scan_state(r, 2)
                decay_sums(t)
                decay_matrix(t, 0)


_INS = ["x", "L0_conv_W_in", "L0_conv_W_conv", "L0_conv_b_conv", "L0_conv_dt_bias", "L0_conv_A_log",
        "L0_conv_D_param", "L0_conv_gamma", "L0_conv_beta", "L0_conv_W_out"]


def kernel(**inputs):
    import numpy as _np
    import concourse.bacc as _bacc
    from concourse import mybir as _mybir
    from concourse.bass_utils import run_bass_kernel_spmd as _run

    nc = _bacc.Bacc("TRN2", target_bir_lowering=False, num_devices=1)
    arrays, args = {}, []
    tiles = lambda v: _np.ascontiguousarray(_np.asarray(v).reshape(MT, 128).T)
    laid = {name: _np.asarray(inputs[name]) for name in _INS[:2]}
    laid["W_conv"] = _np.asarray(inputs["L0_conv_W_conv"]).reshape(9, DI + 2 * NS).T
    laid["b_conv_x"] = tiles(inputs["L0_conv_b_conv"][:DI])
    laid["b_conv_bc"] = _np.asarray(inputs["L0_conv_b_conv"])[DI:, None]
    for name in _INS[4:7]:
        laid[name] = _np.asarray(inputs[name])
    laid["gamma"], laid["beta"] = tiles(inputs["L0_conv_gamma"]), tiles(inputs["L0_conv_beta"])
    laid["W_out"] = _np.asarray(inputs["L0_conv_W_out"])
    for name, a in laid.items():
        a = _np.ascontiguousarray(a)
        arrays[f"in_{name}_dram"] = a
        args.append(nc.dram_tensor(f"in_{name}_dram", a.shape, _mybir.dt.from_np(a.dtype), kind="ExternalInput").ap())
    c = constants()
    arrays["in_consts_dram"] = c
    args.append(nc.dram_tensor("in_consts_dram", c.shape, F32, kind="ExternalInput").ap())
    o = nc.dram_tensor("out_0_dram", (B, H, W, C), F32, kind="ExternalOutput").ap()
    build(nc, *args, o)
    r = _run(nc, [arrays], core_ids=[0])
    return r.results[0]["out_0_dram"]
```

```python
from contextlib import ExitStack

import numpy as np
import concourse.bass as bass
from concourse import mybir

F32 = mybir.dt.float32
F32R = mybir.dt.float32r
ALU = mybir.AluOpType
ACT = mybir.ActivationFunctionType
AX = mybir.AxisListType

B, H, W, C = 8, 64, 64, 384
NG = 32
CG = C // NG
DI = 2 * C
NH, HD, NS = 12, 64, 16
PR = B // 2
TOK = B * W
KC = C // 128
MT = DI // 128
GR = NH // 4
BC = MT
B0, C0, DT0 = 0, 32, 64
BCP = C0 + NS
BCW = DT0 + NH
WIN = 2 * DI + BCW
GN_EPS, LN_EPS = 1e-5, 1e-5
SERIES = [1.0 / (2 * k + 1) for k in range(8)]

IDENT, LATER, UPTO, SAMEIMG, TRI, HEADOF, MHALF, LNEPS = 0, 128, 256, 384, 416, 480, 484, 488
NCONST = 492


def constants():
    k = np.arange(128)[:, None]
    j = np.arange(128)[None, :]
    same = (k // W) == (j // W)
    c = np.zeros((128, NCONST), np.float32)
    c[:, IDENT:IDENT + 128] = k == j
    c[:, LATER:LATER + 128] = same & (k > j)
    c[:, UPTO:UPTO + 128] = same & (k <= j)
    c[:, SAMEIMG:SAMEIMG + 32] = (k // W) == (np.arange(32)[None, :] // NS)
    c[:, TRI:TRI + 64] = (k % W) <= np.arange(64)[None, :]
    c[:, HEADOF:HEADOF + 2] = (k // 32) % 2 == np.arange(2)[None, :]
    c[:, MHALF:MHALF + 4] = -0.5
    c[:, LNEPS:LNEPS + 4] = LN_EPS
    return c


class Row:

    def __init__(self, i, j):
        self.i, self.j = i, j

    def back(self, lag):
        return Row(self.i, self.j - lag)

    @property
    def parity(self):
        return self.j % 2

    @property
    def static(self):
        return isinstance(self.i, int)

    def first(self):
        return self.static and 2 * self.i + self.j == 0

    def last(self):
        return self.static and 2 * self.i + self.j == H - 1

    def exists(self):
        return not self.static or 0 <= 2 * self.i + self.j < H

    def number(self):
        return self.i * 2 + self.j

    def count(self, per_row, k):
        return self.i * (2 * per_row) + (self.j * per_row + k)


PER_ROW = dict(
    z_mm=6, yT_mm=6, xT_mm=3, cv_mm=7, out_mm=4, dtT_mm=1, bcg_mm=1, se_mm=1, xk_mm=6, df_mm=6,
    cet_mm=3, yo_mm=3, y_mm=6, st_mm=3,
    sz=6, ya=6, xh=3, dtv=1, du=2, de=1, bc_act=2, xc_act=6, xk=6, L=6, cet=3, sbd=3, yh=4, bg=7,
    xl=3, tap=42, tapb=14, dch=18, gb=3, yv=6, bst=12, ss=3, agg=4, yn=4, ot=4,
    xn=2, R=6, Mv=6, be=3, ce=3, xd=3, xD=3, sd=3, rs=2, yp=6, ylo=4,
)

FILLS = [
    ("yT", 2, 2, "ya", 3), ("yT", 3, 2, "ya", 4), ("cet", 1, 1, "cet", 2), ("xk", 1, 1, "xk", 2),
    ("yT", 4, 2, "ya", 5), ("st", 0, 1, "ss", 1), ("yT", 5, 2, "ya", 6), ("df", 2, 1, "L", 3),
    ("xk", 2, 1, "xk", 3), ("z", 0, 1, "sz", 1), ("out", 0, 2, "ot", 1), ("out", 1, 2, "ot", 2),
    ("z", 1, 1, "sz", 2), ("xk", 3, 1, "xk", 4), ("df", 3, 1, "L", 4), ("z", 2, 1, "sz", 3),
    ("z", 3, 1, "sz", 4), ("z", 4, 1, "sz", 5), ("z", 5, 1, "sz", 6), ("xk", 4, 1, "xk", 5),
    ("xk", 5, 1, "xk", 6), ("xT", 0, -1, "xl", 1), ("xT", 1, -1, "xl", 2), ("xT", 2, -1, "xl", 3),
    ("df", 4, 1, "L", 5), ("cet", 2, 1, "cet", 3), ("st", 1, 1, "ss", 2), ("df", 5, 1, "L", 6),
    ("dtT", 0, -1, "dch", 1), ("out", 2, 2, "ot", 3), ("df", 0, 0, "L", 1), ("out", 3, 2, "ot", 4),
    ("df", 1, 0, "L", 2), ("bcg", 0, 0, "gb", 3), ("se", 0, 0, "de", 1), ("cet", 0, 0, "cet", 1),
    ("xk", 0, 0, "xk", 1), ("yT", 0, 1, "ya", 1), ("yT", 1, 1, "ya", 2), ("st", 2, 1, "ss", 3),
]
PLACE = {(f[0], f[1]): n for n, f in enumerate(FILLS)}
LAG = {(f[0], f[1]): f[2] for f in FILLS}
assert len(FILLS) % 4 == 0


def build(nc, x, W_in, W_conv, b_conv_x, b_conv_bc, dt_bias, A_log, D_param, gamma, beta, W_out, consts, out):
    with ExitStack() as ctx:
        def sb(name, shape, dt=F32):
            return ctx.enter_context(nc.sbuf_tensor(name, shape, dt))

        def ps(name, shape=(128, 512)):
            return ctx.enter_context(nc.psum_tensor(name, list(shape), F32))

        def semaphore(name):
            return ctx.enter_context(nc.semaphore(name))

        cst = sb("cst", [128, NCONST])
        win_hi = sb("win_hi", [128, KC, WIN], F32R)
        win_lo = sb("win_lo", [128, KC, WIN], F32R)
        wout_hi = sb("wout_hi", [128, MT, C], F32R)
        wout_lo = sb("wout_lo", [128, MT, C], F32R)
        wcv = sb("wcv", [128, MT, 9])
        wcv_bc = sb("wcv_bc", [BCP, 9])
        bcv = sb("bcv", [128, MT])
        bcv_bc = sb("bcv_bc", [BCP, 1])
        gam = sb("gam", [128, MT])
        bet = sb("bet", [128, MT])
        dtb = sb("dtb", [128, NH])
        negA = sb("negA", [128, NH])
        Dp = sb("Dp", [128, NH])
        gn_s = sb("gn_s", [128, PR * NG])
        gn_t = sb("gn_t", [128, PR * NG])
        xt = sb("xt", [128, PR, C])
        xhi = sb("xhi", [128, 2, KC, TOK], F32R)
        xlo = sb("xlo", [128, 2, KC, TOK], F32R)
        acc = sb("acc", [128, 2, MT, TOK])
        acc_bc = sb("acc_bc", [BCP, 2, TOK])
        xc = sb("xc", [128, 2, TOK])
        xc_bc = sb("xc_bc", [BCP, TOK])
        thin = sb("thin", [NS, TOK])
        bcB, bcC, dtv = xc_bc[B0:B0 + NS, :], thin[:, :], thin[0:NH, :]
        sm = sb("sm", [128, 9, PR * NH])
        dt = sb("dt", [128, 2, PR, NH])
        dA = sb("dA", [128, 2, PR, NH])
        dAs = sb("dAs", [128, 2, GR, 2, 2, 8])
        later_r = sb("later_r", [128, 128], F32R)
        DE = sb("DE", [128, 108])
        G = sb("G", [128, PR, W])
        Bbd = sb("Bbd", [128, PR, 2, NS])
        Cbd = sb("Cbd", [128, PR, 2, NS])
        R = sb("R", [128, 2, 8, W], F32R)
        L = sb("L", [128, PR, 4, W])
        BE = sb("BE", [128, PR, 4, 2 * NS])
        CE = sb("CE", [128, PR, 4, 2 * NS])
        CET = sb("CET", [128, PR, 128])
        S = sb("S", [128, GR, PR, HD])
        Sbd = sb("Sbd", [128, PR, 2, HD])
        Xtok = sb("Xtok", [128, 2, PR, 4 * HD])
        Xd = sb("Xd", [128, 2, PR, 4 * HD])
        y = sb("y", [128, PR, DI])
        bst = sb("bst", [128, PR, GR, 6])
        mv = sb("mv", [128, PR, 2])
        vare = sb("vare", [128, PR])
        rstd = sb("rstd", [128, PR])
        ya = sb("ya", [128, TOK])
        yz = sb("yz", [128, MT, TOK])
        yhi = sb("yhi", [128, 2, MT, 128], F32R)
        ylo = sb("ylo", [128, 2, MT, 128], F32R)
        xres = sb("xres", [128, 2, C])

        shared = [ps(f"shared{n}") for n in range(4)]
        cbank = [ps(f"conv{n}") for n in range(2)]
        ybank = [ps(f"ybank{n}") for n in range(2)]

        ident = cst[:, IDENT:IDENT + 128]
        tri = cst[:, TRI:TRI + W]
        sameimg = cst[:, SAMEIMG:SAMEIMG + 32]

        sem = {name: semaphore(name) for name in PER_ROW}
        s_const = semaphore("s_const")
        s_small = semaphore("s_small")
        s_ones = semaphore("s_ones")
        s_wout = semaphore("s_wout")
        s_wosplit = semaphore("s_wosplit")
        s_wst = [semaphore(f"s_wst{k}") for k in range(KC)]
        s_wsplit = semaphore("s_wsplit")
        s_prep = semaphore("s_prep")
        s_init = semaphore("s_init")
        s_chunk = [semaphore(f"s_chunk{c}") for c in range(4)]
        s_sqr = semaphore("s_sqr")
        s_red = semaphore("s_red")
        s_sum = semaphore("s_sum")
        s_tot = semaphore("s_tot")
        s_var = semaphore("s_var")
        s_pow = semaphore("s_pow")
        s_gn = semaphore("s_gn")
        s_last = semaphore("s_last")
        s_xin = semaphore("s_xin")
        s_xr = [semaphore("s_xr0"), semaphore("s_xr1")]
        s_st = [semaphore("s_st0"), semaphore("s_st1")]

        def wait(eng, name, row, k):
            v = row.count(PER_ROW[name], k)
            if isinstance(v, int) and v <= 0:
                return
            eng.wait_ge(sem[name], v)

        def settle(eng):
            eng.nop(nofuse=True)

        def wait_free(eng, row, name, n):
            at = PLACE[name, n]
            t = row.back(-LAG[name, n])
            place, back = at - 4, 0
            while back < 4:
                if place < 0:
                    place, back = place + len(FILLS), back + 1
                _, _, lag, reader, k = FILLS[place]
                row = t.back(back + lag)
                if row.exists():
                    wait(eng, reader, row, k)
                    break
                place -= 4
            return shared[at % 4]

        def bank_of(name, n):
            return shared[PLACE[name, n] % 4]

        def conv_bank(t, tile):
            o = 0 if tile == BC else tile + 1
            return cbank[(t.parity + o) % 2]

        def steps(eng):
            def rows(t):
                return t.back(-1), t, t.back(1), t.back(2)

            for t in range(-1, 4):
                yield rows(Row(t // 2, t % 2))
            with eng.Fori(2, H // 2 - 1) as i:
                for j in range(2):
                    yield rows(Row(i, j))
            for t in range(H - 2, H + 2):
                yield rows(Row(t // 2, t % 2))

        NCHUNK, CTOK = 4, 8
        HALF = CTOK // 2 * C
        PE_CHUNKS = NCHUNK - 1
        RED = 2 * NCHUNK + 2
        VAR = 5
        summed = lambda k: k + 1 if k < 2 else k + 2
        flat3 = "p a b -> p (a b)"
        stage = [y[:, :, :].rearrange(flat3), yz[:, :, :].rearrange(flat3), acc[:, 0].rearrange(flat3),
                 acc[:, 1].rearrange(flat3)]
        squares = [v[:, :, :, :].rearrange("p a b c -> p (a b c)")[:, 0:HALF] for v in (Xtok, Xd)]
        gnw = L[:, :, :, :].rearrange("p a b c -> p (a b c)")
        NI = B * NG
        sum8, var8 = gnw[:, 0:NI], gnw[:, NI:2 * NI]
        mhalf32, ex2, meansq = (gnw[:, 2 * NI + n * NG:2 * NI + (n + 1) * NG] for n in range(3))
        part = gnw[:, 2 * NI + 3 * NG:2 * NI + 5 * NG]
        sq_part = gnw[:, 2 * NI + 5 * NG:2 * NI + (5 + 2 * NCHUNK) * NG].rearrange("p (c g) -> p c g", g=NG)
        wst = [Xtok[:, :, :, :].rearrange("p a b c -> p (a b c)"), stage[2], stage[3]]
        wost = y[:, 0:3].rearrange("p a b -> p (a b)").rearrange("p (m n) -> p m n", n=C)

        def images(eng):
            yield 0, 0
            yield 1, 1
            with eng.Fori(1, B // 2) as i:
                for j in range(2):
                    yield i * 2 + j, j

        xpair = x.rearrange("(p i) h w c -> i h w p c", i=2)

        def row_of(v, i, row):
            return v[i][bass.ds(row.number(), 1)].rearrange("a w p c -> w (a p) c")

        def load_row(eng, row):
            for i in range(2):
                eng.dma_start(xt[64 * i:64 * i + 64], row_of(xpair, i, row)).then_inc(s_xin, 16)

        block = ctx.enter_context(nc.Block())

        @block.sync
        def _(sp):
            sp.dma_start(cst[:, :], consts[:, :]).then_inc(s_const, 16)
            for k in range(KC):
                sp.dma_start(wst[k][:, 0:W_in.shape[1]], W_in[128 * k:128 * k + 128, :]).then_inc(s_wst[k], 16)

            xi = x.rearrange("b h w c -> b (h w c)").rearrange("b (p n) -> b p n", p=128)

            def load_chunk(im, c):
                if not (isinstance(im, int) and im == 0):
                    sp.wait_ge(s_sqr, (im - 1) * (2 * NCHUNK) + 2 * (c + 1))
                    settle(sp)
                    if c:
                        sp.wait_ge(s_sum, (im - 1) * PE_CHUNKS + c)
                    else:
                        sp.wait_ge(s_red, (im - 1) * RED + 3)
                elif c >= 2:
                    sp.wait_ge(s_wsplit, 8 * c)
                sp.dma_start(stage[c], xi[im, :, c * CTOK * C:(c + 1) * CTOK * C]).then_inc(s_chunk[c], 16)

            for im, _ in images(sp):
                for c in range(NCHUNK):
                    if isinstance(im, int) and im == 0 and c == 2:
                        sp.dma_start(wcv[:, :, :], W_conv[0:DI, :].rearrange("(m p) k -> p m k", p=128)).then_inc(s_small, 16)
                        sp.dma_start(bcv[:, :], b_conv_x[:, :]).then_inc(s_small, 16)
                        sp.wait_ge(s_init, 2)
                        for at, n in ((B0, DI), (C0, DI + NS)):
                            sp.dma_start(wcv_bc[at:at + NS, :], W_conv[n:n + NS, :]).then_inc(s_small, 16)
                            sp.dma_start(bcv_bc[at:at + NS, :], b_conv_bc[n - DI:n - DI + NS, :]).then_inc(s_small, 16)
                        sp.dma_start(gam[:, :], gamma[:, :]).then_inc(s_small, 16)
                        sp.dma_start(bet[:, :], beta[:, :]).then_inc(s_small, 16)
                        for dst, v in ((dtb, dt_bias), (negA, A_log), (Dp, D_param)):
                            sp.dma_start(dst[:, :], v.rearrange("(a h) -> a h", a=1).to_broadcast([128, NH])).then_inc(s_small, 16)
                    load_chunk(im, c)

            sp.wait_ge(s_sqr, (B - 1) * (2 * NCHUNK) + 2)
            sp.wait_ge(s_red, (B - 1) * RED + 3)
            sp.dma_start(wost, W_out.rearrange("(m p) n -> p m n", p=128)).then_inc(s_wout, 16)

            opair = out.rearrange("(p i) h w c -> i h w p c", i=2)

            def load_residual(row, p):
                v = row.count(64, 32 * (p // 2))
                if not (isinstance(v, int) and v <= 0):
                    sp.wait_ge(s_st[p % 2], v)
                for i in range(2):
                    sp.dma_start(xres[64 * i:64 * i + 64, p % 2], row_of(xpair, i, row)[:, p]).then_inc(s_xr[p % 2], 16)

            load_row(sp, Row(0, 0))
            for n, t, r, q in steps(sp):
                if q.exists():
                    for p in range(2):
                        load_residual(q, p)
                    for p in range(PR):
                        wait(sp, "ot", q, p + 1)
                        for i in range(2):
                            sp.dma_start(row_of(opair, i, q)[:, p], xres[64 * i:64 * i + 64, p % 2]).then_inc(s_st[p % 2], 16)
                        if p < 2:
                            load_residual(q, p + 2)
            for s in range(2):
                sp.wait_ge(s_st[s], 64 * H)

        @block.gpsimd
        def _(pool):
            pool.memset(mhalf32, -0.5).then_inc(s_pow, 1)
            pool.wait_ge(s_pow, 1)
            for im, _ in images(pool):
                pool.wait_ge(s_var, im * VAR + VAR)
                v = var8[:, bass.ds(im * NG, NG)]
                pool.tensor_tensor(v, v, mhalf32, ALU.pow).then_inc(s_pow, 1)

            pool.wait_ge(s_const, 16)
            pool.wait_ge(s_small, 16 * 11)
            pool.wait_ge(s_prep, 2)
            pool.wait_ge(s_gn, 4)
            pool.wait_ge(s_init, 6)

            def scale_row(n):
                if not n.exists():
                    return
                v = xt[:, :, :].rearrange("p a (g c) -> p (a g) c", c=CG)
                pool.wait_ge(s_xin, n.count(32, 32))
                pool.tensor_tensor(v, v, gn_s[:, :].unsqueeze(2).to_broadcast([128, PR * NG, CG]), ALU.mult).then_inc(sem["xn"], 1)

            def shift_row(n):
                if not n.exists():
                    return
                v = xt[:, :, :].rearrange("p a (g c) -> p (a g) c", c=CG)
                wait(pool, "xn", n, 1)
                pool.tensor_tensor(v, v, gn_t[:, :].unsqueeze(2).to_broadcast([128, PR * NG, CG]), ALU.add).then_inc(sem["xn"], 1)

            def decay_steps(r, m):
                if not r.exists():
                    return
                g, b = m // 2, m % 2
                wait(pool, "dch", r, 18)
                wait(pool, "df_mm", r, m)
                a = dAs[:, r.parity, g, b].rearrange("p s h -> p (s h)").unsqueeze(2).to_broadcast([128, 16, W])
                pool.tensor_tensor(R[:, :, :, :].rearrange("p s h l -> p (s h) l"), a,
                                   tri.unsqueeze(1).to_broadcast([128, 16, W]), ALU.mult).then_inc(sem["R"], 1)

            def scale_BC(r, g, name):
                if not r.exists():
                    return
                wait(pool, "gb", r, 3)
                wait(pool, "de", r, 1)
                dst, src, e, reader = {"be": (BE, Bbd, 0, "st_mm"), "ce": (CE, Cbd, 1, "cet_mm")}[name]
                wait(pool, reader, r, g)
                d = DE[:, 0:96].rearrange("p (e a h) -> p e a h", e=2, a=PR)
                v = src[:, :, :, :].rearrange("p a i n -> p a (i n)").unsqueeze(2).to_broadcast([128, PR, 4, 2 * NS])
                w = d[:, e, :, 4 * g:4 * g + 4].unsqueeze(3).to_broadcast([128, PR, 4, 2 * NS])
                pool.tensor_tensor(dst[:, :, :, :], v, w, ALU.mult).then_inc(sem[name], 1)

            def masked(r, g):
                if not r.exists():
                    return
                for b in range(2):
                    wait(pool, "L", r, 2 * g + b + 1)
                    wait(pool, "gb", r, 1)
                    v = L[:, 2 * b:2 * b + 2]
                    pool.tensor_tensor(v, v, G[:, 2 * b:2 * b + 2].unsqueeze(2).to_broadcast([128, 2, 4, W]),
                                       ALU.mult).then_inc(sem["Mv"], 1)

            def x_dt(r, g):
                if not r.exists():
                    return
                slot = (r.parity + g) % 2
                wait(pool, "dch", r, 15)
                wait(pool, "xk", r, 2 * g + 2)
                wait(pool, "st_mm", r, g - 1)
                wait(pool, "y_mm", r, 2 * g - 2)
                w = dt[:, r.parity, :, 4 * g:4 * g + 4].unsqueeze(3).to_broadcast([128, PR, 4, HD])
                pool.tensor_tensor(Xd[:, slot].rearrange("p a (h d) -> p a h d", h=4),
                                   Xtok[:, slot].rearrange("p a (h d) -> p a h d", h=4), w, ALU.mult).then_inc(sem["xd"], 1)

            def x_D(r, g):
                if not r.exists():
                    return
                xv = Xtok[:, (r.parity + g) % 2].rearrange("p a (h d) -> p a h d", h=4)
                wait(pool, "xd", r, g + 1)
                w = Dp[:, 4 * g:4 * g + 4].unsqueeze(1).unsqueeze(3).to_broadcast([128, PR, 4, HD])
                pool.tensor_tensor(xv, xv, w, ALU.mult).then_inc(sem["xD"], 1)

            def decay_state(r, g):
                if not r.exists():
                    return
                wait(pool, "sbd", r, g + 1)
                wait(pool, "de", r, 1)
                dec = DE[:, 96:108].rearrange("p (a g) -> p a g", a=PR)[:, :, g].unsqueeze(2).to_broadcast([128, PR, HD])
                pool.tensor_tensor(S[:, g], S[:, g], dec, ALU.mult).then_inc(sem["sd"], 1)

            def ln_scale(q):
                if not q.exists():
                    return
                wait(pool, "agg", q, 4)
                pool.tensor_tensor(vare[:, :], mv[:, :, 1], cst[:, LNEPS:LNEPS + PR], ALU.add).then_inc(sem["rs"], 1)
                wait(pool, "rs", q, 1)
                pool.tensor_tensor(rstd[:, :], vare[:, :], cst[:, MHALF:MHALF + PR], ALU.pow).then_inc(sem["rs"], 1)

            def gated(q, m):
                if not q.exists():
                    return
                wait(pool, "ya", q, m + 1)
                wait(pool, "sz", q, m + 1)
                pool.tensor_tensor(yz[:, m], ya[:, :], yz[:, m], ALU.mult).then_inc(sem["yp"], 1)

            def gated_low(q, p):
                if not q.exists():
                    return
                wait(pool, "yh", q, p + 1)
                pool.tensor_tensor(ylo[:, p % 2], yz[:, :, 128 * p:128 * p + 128], yhi[:, p % 2].bitcast(F32),
                                   ALU.subtract).then_inc(sem["ylo"], 1)

            for n, t, r, q in steps(pool):
                x_D(q, 2)
                masked(q, 2)
                scale_BC(q, 2, "be")
                decay_steps(r, 0)
                scale_row(n)
                decay_steps(r, 1)
                ln_scale(q)
                decay_steps(r, 2)
                scale_BC(r, 0, "ce")
                masked(r, 0)
                gated(q, 0)
                scale_BC(r, 1, "ce")
                gated(q, 1)
                scale_BC(r, 0, "be")
                gated(q, 2)
                x_dt(r, 0)
                decay_state(r, 0)
                gated(q, 3)
                x_D(r, 0)
                for m in range(4, 6):
                    gated(q, m)
                scale_BC(r, 1, "be")
                for m in range(0, 2):
                    gated_low(q, m)
                decay_steps(r, 3)
                gated_low(q, 2)
                scale_BC(r, 2, "ce")
                gated_low(q, 3)
                shift_row(n)
                masked(r, 1)
                x_dt(r, 1)
                x_D(r, 1)
                decay_state(r, 1)
                decay_steps(r, 4)
                x_dt(r, 2)
                decay_steps(r, 5)
                decay_state(r, 2)

        @block.scalar
        def _(act):
            for im, _ in images(act):
                for k in range(2 * NCHUNK):
                    act.wait_ge(s_chunk[k // 2], im * 16 + 16)
                    if isinstance(im, int) and im == 0 and k == 0:
                        act.wait_ge(s_wsplit, 8)
                    if not (isinstance(im, int) and im == 0 and k < 2):
                        act.wait_ge(s_red, im * RED + summed(k - 2) if k >= 2 else (im - 1) * RED + summed(2 * NCHUNK - 2 + k))
                    act.activation(squares[k % 2], stage[k // 2][:, (k % 2) * HALF:(k % 2 + 1) * HALF], ACT.Square).then_inc(s_sqr, 1)

            act.wait_ge(s_const, 16)
            act.wait_ge(s_small, 16 * 11)
            act.activation(negA[:, :], negA[:, :], ACT.Exp).then_inc(s_prep, 1)
            act.wait_ge(s_prep, 1)
            act.mul(negA[:, :], negA[:, :], -1.0).then_inc(s_prep, 1)

            def gate(r, m):
                if not r.exists():
                    return
                wait(act, "z_mm", r, m + 1)
                wait(act, "ylo", r, 0)
                act.activation(yz[:, m], bank_of("z", m)[:, :], ACT.Silu).then_inc(sem["sz"], 1)

            def affine(q, m):
                if not q.exists():
                    return
                wait(act, "yT_mm", q, m + 1)
                wait(act, "yp", q, m)
                act.activation(ya[:, :], bank_of("yT", m)[:, :], ACT.Identity, bias=bet[:, m:m + 1],
                               scale=gam[:, m:m + 1]).then_inc(sem["ya"], 1)

            def gated_high(q, p):
                if not q.exists():
                    return
                wait(act, "yp", q, 6)
                wait(act, "out_mm", q, p - 1)
                act.activation(yhi[:, p % 2], yz[:, :, 128 * p:128 * p + 128], ACT.Copy).then_inc(sem["yh"], 1)

            def x_hi(n, k):
                if not n.exists():
                    return
                wait(act, "xT_mm", n, k + 1)
                wait(act, "z_mm", n.back(2), 6)
                wait(act, "cv_mm", n.back(2), 7)
                act.activation(xhi[:, n.parity, k], bank_of("xT", k)[:, :], ACT.Copy).then_inc(sem["xh"], 1)
                if k == KC - 1 and n.back(-1).exists():
                    load_row(act, n.back(-1))

            def take_dt(t):
                if not t.exists():
                    return
                wait(act, "cv_mm", t, 1)
                wait(act, "bcg_mm", t.back(1), 0)
                act.activation(dtv, conv_bank(t, BC)[DT0:DT0 + NH, :], ACT.Copy).then_inc(sem["dtv"], 1)

            def silu_bc(r):
                if not r.exists():
                    return
                if r.last():
                    act.wait_ge(s_last, 1)
                else:
                    wait(act, "tap", r.back(-1), 5)
                    wait(act, "dtT_mm", r.back(-1), 1)
                wait(act, "bcg_mm", r, 0)
                act.activation(bcB, bcB, ACT.Silu).then_inc(sem["bc_act"], 1)
                act.activation(bcC, xc_bc[C0:C0 + NS, :], ACT.Silu).then_inc(sem["bc_act"], 1)

            def decays(r):
                if not r.exists():
                    return
                wait(act, "se_mm", r, 1)
                wait(act, "be", r, 0)
                wait(act, "ce", r, 0)
                wait(act, "sd", r, 0)
                act.activation(DE[:, :], bank_of("se", 0)[:, 0:108], ACT.Exp).then_inc(sem["de"], 1)

            def begin_row(t, tile):
                if not t.exists():
                    return
                o = 0 if tile == BC else tile + 1
                wait(act, "tap", t, 6 * o + 6)
                if tile == BC:
                    act.activation(acc_bc[:, (t.parity + 1) % 2], conv_bank(t, BC)[0:BCP, :], ACT.Identity, bias=bcv_bc[:, 0:1],
                                   scale=wcv_bc[:, 1:2]).then_inc(sem["bg"], 1)
                else:
                    act.activation(acc[:, (t.parity + 1) % 2, tile], conv_bank(t, tile)[:, :], ACT.Identity,
                                   bias=bcv[:, tile:tile + 1], scale=wcv[:, tile, 1:2]).then_inc(sem["bg"], 1)

            def silu_conv(r, j):
                if not r.exists():
                    return
                if r.last():
                    act.wait_ge(s_last, j + 2)
                else:
                    wait(act, "tap", r.back(-1), 6 * (j + 1) + 5)
                act.activation(xc[:, j % 2], xc[:, j % 2], ACT.Silu).then_inc(sem["xc_act"], 1)

            def take_x(r, j):
                if not r.exists():
                    return
                g = j // 2
                wait(act, "xk_mm", r, j + 1)
                wait(act, "yv", r, 2 * g - 2)
                wait(act, "xd", r, g - 1)
                src = bank_of("xk", j)[:, :].rearrange("p (a c) -> p a c", a=PR)
                act.activation(Xtok[:, (r.parity + g) % 2, :, 128 * (j % 2):128 * (j % 2) + 128], src,
                               ACT.Copy).then_inc(sem["xk"], 1)

            def state_blocks(r, g):
                if not r.exists():
                    return
                wait(act, "ss", r.back(1), g + 1)
                wait(act, "yo_mm", r, g)
                for h in range(2):
                    last = act.activation(Sbd[:, :, h], S[:, g], ACT.Copy, scale=cst[:, HEADOF + h:HEADOF + h + 1])
                last.then_inc(sem["sbd"], 1)

            def exp_decay(r, m):
                if not r.exists():
                    return
                b = m % 2
                wait(act, "df_mm", r, m + 1)
                wait(act, "y_mm", r, 2 * (m // 2))
                src = bank_of("df", m)[:, :].rearrange("p (a h l) -> p a h l", a=2, h=4)
                act.activation(L[:, 2 * b:2 * b + 2], src, ACT.Exp).then_inc(sem["L"], 1)

            def take_cet(r, g):
                if not r.exists():
                    return
                wait(act, "cet_mm", r, g + 1)
                wait(act, "yo_mm", r, g)
                act.activation(CET[:, :, :], bank_of("cet", g)[:, :].rearrange("p (a l) -> p a l", a=PR),
                               ACT.Copy).then_inc(sem["cet"], 1)

            def softplus_exp(t):
                if not t.exists():
                    return
                wait(act, "dch", t, 1)
                act.activation(sm[:, 1], sm[:, 0], ACT.Abs).then_inc(sem["du"], 1)
                wait(act, "du", t, 1)
                act.activation(sm[:, 2], sm[:, 1], ACT.Exp, scale=-1.0).then_inc(sem["du"], 1)

            act.wait_ge(s_init, 6)
            act.wait_ge(s_gn, 4)
            for n, t, r, q in steps(act):
                state_blocks(q, 2)
                begin_row(r, 5)
                silu_conv(q, 5)
                gate(q, 3)
                take_x(q, 4)
                for m in range(4, 6):
                    gate(q, m)
                take_x(q, 5)
                for m in range(0, 3):
                    x_hi(t, m)
                exp_decay(q, 4)
                take_dt(t)
                exp_decay(q, 5)
                take_cet(q, 2)
                silu_bc(r)
                begin_row(t, BC)
                exp_decay(r, 0)
                state_blocks(r, 0)
                begin_row(t, 0)
                exp_decay(r, 1)
                softplus_exp(t)
                decays(r)
                silu_conv(r, 0)
                affine(q, 0)
                take_x(r, 0)
                take_cet(r, 0)
                affine(q, 1)
                silu_conv(r, 1)
                begin_row(t, 1)
                affine(q, 2)
                take_x(r, 1)
                take_cet(r, 1)
                for m in range(3, 5):
                    affine(q, m)
                begin_row(t, 2)
                silu_conv(r, 2)
                affine(q, 5)
                state_blocks(r, 1)
                gated_high(q, 0)
                exp_decay(r, 2)
                gated_high(q, 1)
                take_x(r, 2)
                silu_conv(r, 3)
                gated_high(q, 2)
                begin_row(t, 3)
                gated_high(q, 3)
                begin_row(t, 4)
                for m in range(0, 2):
                    gate(r, m)
                exp_decay(r, 3)
                take_x(r, 3)
                gate(r, 2)
                silu_conv(r, 4)

        @block.vector
        def _(dve):
            dve.memset(ya[:, 0:128], 1.0).then_inc(s_ones, 1)
            dve.memset(wcv_bc[:, :], 0.0).then_inc(s_init, 1)
            dve.memset(bcv_bc[:, :], 0.0).then_inc(s_init, 1)
            for w in (win_hi, win_lo):
                dve.memset(w[:, :, 2 * DI:WIN].bitcast(F32), 0.0).then_inc(s_init, 1)
            dve.memset(S[:, :, :, :], 0.0).then_inc(s_init, 1)
            dve.wait_ge(s_init, 5)
            spans = [(0, 2 * DI, 0), (2 * DI, 2 * DI + NS, 2 * DI + B0), (2 * DI + NS, 2 * DI + 2 * NS, 2 * DI + C0),
                     (2 * DI + 2 * NS, 2 * DI + 2 * NS + NH, 2 * DI + DT0)]
            for k in range(KC):
                dve.wait_ge(s_wst[k], 16)
                for n, (a, b, at) in enumerate(spans):
                    dve.tensor_copy(win_hi[:, k, at:at + b - a], wst[k][:, a:b]).then_inc(s_wsplit, 1)
                dve.wait_ge(s_wsplit, 8 * k + 4)
                for n, (a, b, at) in enumerate(spans):
                    dve.tensor_tensor(win_lo[:, k, at:at + b - a], wst[k][:, a:b],
                                      win_hi[:, k, at:at + b - a].bitcast(F32), ALU.subtract).then_inc(s_wsplit, 1)

            dve.wait_ge(s_const, 16)
            dve.tensor_copy(later_r[:, :], cst[:, LATER:LATER + 128]).then_inc(s_init, 1)

            by_group = "p (n g c) -> p g n c"

            def sum_squares(im, k):
                dve.wait_ge(s_sqr, im * (2 * NCHUNK) + (k + 1))
                dve.tensor_reduce(sq_part[:, k], squares[k % 2].rearrange(by_group, g=NG, c=CG), AX.XY, ALU.add).then_inc(s_red, 1)

            def variance(im, par):
                total, at = sum8[:, bass.ds(im * NG, NG)], im * VAR
                dve.wait_ge(s_tot, im + 1)
                dve.tensor_reduce(total, ybank[par][:, 0:C].rearrange("p (g c) -> p g c", c=CG), AX.X, ALU.add).then_inc(s_var, 1)
                if not (isinstance(im, int) and im == 0):
                    dve.wait_ge(s_var, at)
                dve.tensor_scalar(ex2, cbank[par][:, NG:2 * NG], 1.0 / (H * W * CG), GN_EPS, ALU.mult, ALU.add).then_inc(s_var, 1)
                dve.wait_ge(s_var, at + 1)
                dve.tensor_tensor(total, cbank[par][:, 0:NG], total, ALU.add).then_inc(s_var, 1)
                dve.wait_ge(s_var, at + 3)
                dve.scalar_tensor_tensor(out=meansq, in0=total, scalar=-1.0 / (H * W * CG) ** 2, in1=total, op0=ALU.mult,
                                         op1=ALU.mult).then_inc(s_var, 1)
                dve.wait_ge(s_var, at + 4)
                dve.tensor_tensor(var8[:, bass.ds(im * NG, NG)], ex2, meansq, ALU.add).then_inc(s_var, 1)

            for im, par in images(dve):
                first = isinstance(im, int) and im == 0
                for k in range(2 * NCHUNK):
                    if k == 0 and not first:
                        dve.wait_ge(s_red, im * RED)
                    sum_squares(im, k)
                    if k == 1:
                        if not first:
                            dve.wait_ge(s_tot, im)
                        dve.tensor_reduce(part[:, 0:NG], stage[0].rearrange(by_group, g=NG, c=CG), AX.XY, ALU.add).then_inc(s_red, 1)
                        if not first:
                            variance(im - 1, 1 - par)
                dve.wait_ge(s_red, im * RED + RED - 1)
                dve.tensor_reduce(part[:, NG:2 * NG], sq_part.rearrange("p c g -> p g c"), AX.X, ALU.add).then_inc(s_red, 1)
            variance(B - 1, 1)
            dve.wait_ge(s_wout, 16)
            dve.tensor_copy(wout_hi[:, :, :], wost).then_inc(s_wosplit, 1)
            dve.wait_ge(s_wosplit, 1)
            dve.tensor_tensor(wout_lo[:, :, :], wost, wout_hi[:, :, :].bitcast(F32), ALU.subtract).then_inc(s_wosplit, 1)
            dve.wait_ge(s_pow, 1 + B)
            dve.wait_ge(s_var, B * VAR)
            dve.scalar_tensor_tensor(out=sum8, in0=sum8, scalar=-1.0 / (H * W * CG), in1=var8, op0=ALU.mult,
                                     op1=ALU.mult).then_inc(s_var, 1)
            dve.wait_ge(s_var, B * VAR + 1)
            for dst, src in ((gn_s, var8), (gn_t, sum8)):
                v = src.rearrange("p (a i g) -> p a i g", i=2, g=NG)
                for i in range(2):
                    dve.tensor_copy(dst[64 * i:64 * i + 64, :].rearrange("p (a g) -> p a g", g=NG),
                                    v[64 * i:64 * i + 64, :, i]).then_inc(s_gn, 1)
            dve.wait_ge(s_small, 16 * 11)

            dve.memset(acc[:, 1], 0.0).then_inc(s_init, 1)
            dve.memset(acc_bc[:, 1], 0.0).then_inc(s_init, 1)
            dve.wait_ge(s_init, 8)
            for m in range(MT):
                ins = dve.tensor_scalar(acc[:, 0, m], acc[:, 1, m], bcv[:, m:m + 1], None, ALU.add)
                if m < MT - 2:
                    ins.then_inc(s_init, 1)
            dve.tensor_scalar(acc_bc[:, 0], acc_bc[:, 1], bcv_bc[:, 0:1], None, ALU.add).then_inc(s_init, 1)
            dve.wait_ge(s_init, 13)
            dve.wait_ge(s_wosplit, 2)

            def taps(t, tile, part, between=None):
                o = 0 if tile == BC else tile + 1
                bank = conv_bank(t, tile)
                if tile == BC:
                    src, done, this, w = bank[0:BCP, :], acc_bc[:, (t.parity + 1) % 2], acc_bc[:, t.parity], wcv_bc
                    dst, tap = xc_bc[:, :], lambda ky, kx: w[:, 3 * ky + kx:3 * ky + kx + 1]
                else:
                    src, done, this, w = bank[:, :], acc[:, (t.parity + 1) % 2, tile], acc[:, t.parity, tile], wcv
                    dst, tap = xc[:, tile % 2], lambda ky, kx: w[:, tile, 3 * ky + kx:3 * ky + kx + 1]
                s3, d3, a3 = (v.rearrange("p (b w) -> p b w", w=W) for v in (src, done, this))
                begun = d3

                def left(a, ky):
                    return dve.scalar_tensor_tensor(out=a[:, :, 1:W], in0=s3[:, :, 0:W - 1], scalar=tap(ky, 0),
                                                    in1=a[:, :, 1:W], op0=ALU.mult, op1=ALU.add)

                def right(a, ky):
                    return dve.scalar_tensor_tensor(out=a[:, :, 0:W - 1], in0=s3[:, :, 1:W], scalar=tap(ky, 2),
                                                    in1=a[:, :, 0:W - 1], op0=ALU.mult, op1=ALU.add)

                def fill(n):
                    if between is not None:
                        between(n)

                if part == 0:
                    wait(dve, "cv_mm", t, o + 1)
                    wait(dve, "tap", t.back(1), 6 * o + 6)
                    left(d3, 2).then_inc(sem["tap"], 1)
                    fill(0)
                    wait(dve, "tapb", t.back(1), 2 * o + 2)
                    left(a3, 1).then_inc(sem["tap"], 1)
                    fill(1)
                    wait(dve, "tap", t, 6 * o + 1)
                    right(d3, 2).then_inc(sem["tap"], 1)
                    fill(2)
                    wait(dve, "tap", t, 6 * o + 2)
                    right(a3, 1).then_inc(sem["tap"], 1)
                    fill(3)
                    if tile == BC:
                        wait(dve, "bcg_mm", t.back(1), 0)
                    else:
                        wait(dve, "xk_mm", t.back(1), tile - 1)
                    wait(dve, "tap", t, 6 * o + 3)
                    dve.scalar_tensor_tensor(out=dst, in0=src, scalar=tap(2, 1), in1=done, op0=ALU.mult,
                                             op1=ALU.add).then_inc(sem["tap"], 1)
                    fill(4)
                    wait(dve, "tap", t, 6 * o + 4)
                    dve.scalar_tensor_tensor(out=this, in0=src, scalar=tap(1, 1), in1=this, op0=ALU.mult,
                                             op1=ALU.add).then_inc(sem["tap"], 1)
                    fill(5)
                else:
                    wait(dve, "bg", t, o + 1)
                    left(begun, 0).then_inc(sem["tapb"], 1)
                    fill(6)
                    wait(dve, "tapb", t, 2 * o + 1)
                    right(begun, 0).then_inc(sem["tapb"], 1)
                    fill(7)

            def last_row(r, tile):
                wait(dve, "tap", r, 42)
                if tile == BC:
                    wait(dve, "bcg_mm", r, 0)
                    dve.tensor_copy(xc_bc[:, :], acc_bc[:, r.parity]).then_inc(s_last, 1)
                else:
                    wait(dve, "xk_mm", r, tile - 1)
                    dve.tensor_copy(xc[:, tile % 2], acc[:, r.parity, tile]).then_inc(s_last, 1)

            def softplus_step(t, n):
                v, u, w2, rw, q, s, p, lp, vr = (sm[:, n_] for n_ in (0, 2, 3, 4, 5, 6, 7, 8, 1))
                d = dt[:, t.parity].rearrange("p a h -> p (a h)")

                def done(ins):
                    ins.then_inc(sem["dch"], 1)

                if n == 1:
                    wait(dve, "du", t, 2)
                else:
                    wait(dve, "dch", t, n)
                if n == 1:
                    done(dve.tensor_scalar(w2, u, 2.0, None, ALU.add))
                elif n == 2:
                    done(dve.reciprocal(rw, w2))
                elif n == 3:
                    done(dve.tensor_tensor(q, u, rw, ALU.mult))
                elif n == 4:
                    done(dve.tensor_tensor(s, q, q, ALU.mult))
                elif n == 5:
                    done(dve.tensor_scalar(p, s, SERIES[7], None, ALU.mult))
                elif n <= 11:
                    done(dve.scalar_tensor_tensor(out=p, in0=p, scalar=SERIES[12 - n], in1=s, op0=ALU.add, op1=ALU.mult))
                elif n == 12:
                    done(dve.scalar_tensor_tensor(out=lp, in0=p, scalar=1.0, in1=q, op0=ALU.add, op1=ALU.mult))
                elif n == 13:
                    done(dve.tensor_scalar(vr, v, 0.0, None, ALU.max))
                elif n == 14:
                    wait(dve, "xd", t.back(1), 0)
                    wait(dve, "se_mm", t.back(1), 0)
                    done(dve.scalar_tensor_tensor(out=d, in0=lp, scalar=2.0, in1=vr, op0=ALU.mult, op1=ALU.add))
                elif n == 15:
                    done(dve.tensor_tensor(dA[:, t.parity], dt[:, t.parity],
                                           negA[:, :].unsqueeze(1).to_broadcast([128, PR, NH]), ALU.mult))
                else:
                    wait(dve, "R", t.back(1), 0)
                    for g in range(GR):
                        a = dA[:, t.parity].rearrange("p (b a) (g h) -> p g b a h", b=2, h=4)[:, g]
                        hi, lo = (dAs[:, t.parity, g, :, s_].rearrange("p b (a h) -> p b a h", h=4) for s_ in range(2))
                        if n == 16:
                            ins = dve.tensor_copy(hi.bitcast(F32R), a)
                        else:
                            ins = dve.tensor_tensor(lo, a, hi, ALU.subtract)
                    done(ins)

            def conv_part(t, tile, part):
                if t.exists():
                    between = {4: lambda n: softplus_step(t, n) if n else None,
                               5: lambda n: softplus_step(t, n + 8)}.get(tile)
                    taps(t, tile, part, between)
                    if (tile, part) == (5, 1):
                        for n in (16, 17):
                            softplus_step(t, n)
                elif part == 0 and t.back(1).exists():
                    last_row(t.back(1), tile)

            def add_bias(t):
                if not t.exists():
                    return
                wait(dve, "dtT_mm", t, 1)
                dve.tensor_tensor(sm[:, 0].rearrange("p (a h) -> p a h", a=PR),
                                  bank_of("dtT", 0)[:, 0:PR * NH].rearrange("p (a h) -> p a h", a=PR),
                                  dtb[:, :].unsqueeze(1).to_broadcast([128, PR, NH]), ALU.add).then_inc(sem["dch"], 1)

            def residual(q, p):
                if not q.exists():
                    return
                wait(dve, "out_mm", q, p + 1)
                dve.wait_ge(s_xr[p % 2], q.count(64, 32 * (p // 2) + 32))
                dve.tensor_tensor(xres[:, p % 2], bank_of("out", p)[:, 0:C], xres[:, p % 2], ALU.add).then_inc(sem["ot"], 1)

            def take_y(r, g):
                if not r.exists():
                    return
                slot = (r.parity + g) % 2
                wait(dve, "y_mm", r, 2 * g + 2)
                wait(dve, "xD", r, g + 1)
                wait(dve, "yT_mm", r.back(1), 2 * g + 2)
                for b in range(2):
                    at = 256 * g + 128 * b
                    dve.tensor_tensor(y[:, :, at:at + 128], ybank[b][:, :].rearrange("p (a c) -> p a c", a=PR),
                                      Xtok[:, slot, :, 128 * b:128 * b + 128], ALU.add).then_inc(sem["yv"], 1)
                wait(dve, "yv", r, 2 * g + 2)
                for p in range(PR):
                    dve.bn_stats(bst[:, p, g], y[:, p, 256 * g:256 * g + 256]).then_inc(sem["bst"], 1)

            def new_state(r, g):
                if not r.exists():
                    return
                wait(dve, "st_mm", r, g + 1)
                wait(dve, "sd", r, g + 1)
                dve.tensor_tensor(S[:, g], bank_of("st", g)[:, 0:256].rearrange("p (a d) -> p a d", a=PR), S[:, g],
                                  ALU.add).then_inc(sem["ss"], 1)

            def ln_statistics(q):
                if not q.exists():
                    return
                wait(dve, "bst", q, 12)
                settle(dve)
                for p in range(PR):
                    dve.bn_aggr(mv[:, p], bst[:, p].rearrange("p g s -> p (g s)")).then_inc(sem["agg"], 1)

            def ln_normalise(q):
                if not q.exists():
                    return
                wait(dve, "rs", q, 2)
                for p in range(PR):
                    dve.tensor_scalar(y[:, p], y[:, p], mv[:, p, 0:1], rstd[:, p:p + 1], ALU.subtract,
                                      ALU.mult).then_inc(sem["yn"], 1)

            def x_low(n, k):
                if not n.exists():
                    return
                wait(dve, "xh", n, k + 1)
                dve.tensor_tensor(xlo[:, n.parity, k], bank_of("xT", k)[:, :], xhi[:, n.parity, k].bitcast(F32),
                                  ALU.subtract).then_inc(sem["xl"], 1)

            def b_and_c_tokens(r):
                if not r.exists():
                    return
                wait(dve, "bcg_mm", r, 1)
                wait(dve, "Mv", r, 0)
                wait(dve, "be", r, 0)
                wait(dve, "ce", r, 0)
                bank = bank_of("bcg", 0)
                dve.tensor_tensor(G[:, :, :], bank[:, 0:256].rearrange("p (a l) -> p a l", a=PR),
                                  tri.unsqueeze(1).to_broadcast([128, PR, W]), ALU.mult).then_inc(sem["gb"], 1)
                for m, dst in enumerate((Bbd, Cbd)):
                    v = bank[:, 256 + 64 * m:320 + 64 * m].rearrange("p (a n) -> p a n", a=PR).unsqueeze(2)
                    dve.tensor_tensor(dst[:, :, :, :], v.to_broadcast([128, PR, 2, NS]),
                                      sameimg.rearrange("p (i n) -> p i n", i=2).unsqueeze(1).to_broadcast([128, PR, 2, NS]),
                                      ALU.mult).then_inc(sem["gb"], 1)

            for n, t, r, q in steps(dve):
                conv_part(t, 5, 0)
                conv_part(t, 5, 1)
                for m in range(0, 3):
                    x_low(n, m)
                take_y(r, 1)
                conv_part(n, BC, 0)
                conv_part(n, 0, 0)
                new_state(r, 1)
                residual(q, 2)
                add_bias(n)
                conv_part(n, BC, 1)
                take_y(r, 2)
                ln_statistics(r)
                conv_part(n, 0, 1)
                residual(q, 3)
                b_and_c_tokens(t)
                ln_normalise(r)
                conv_part(n, 1, 0)
                new_state(r, 2)
                conv_part(n, 1, 1)
                conv_part(n, 2, 0)
                new_state(t, 0)
                conv_part(n, 2, 1)
                take_y(t, 0)
                conv_part(n, 3, 0)
                conv_part(n, 4, 0)
                residual(r, 0)
                conv_part(n, 3, 1)
                residual(r, 1)
                conv_part(n, 4, 1)

        @block.tensor
        def _(pe):
            pe.wait_ge(s_ones, 1)
            ones = ya[:, 0:128]

            def sum_chunk(im, par, c):
                pe.wait_ge(s_chunk[c], im * 16 + 16)
                for n in range(CTOK):
                    last = pe.matmul(ybank[par][:, 0:C], ones, stage[c][:, n * C:(n + 1) * C],
                                     start=(c == 1 and n == 0), stop=(c == NCHUNK - 1 and n == CTOK - 1))
                last.then_inc(s_sum, 1)

            def sum_partitions(im, par):
                pe.wait_ge(s_red, im * RED + RED)
                pe.matmul(cbank[par][:, 0:2 * NG], ones, part, start=True, stop=True).then_inc(s_tot, 1)

            for im, par in images(pe):
                static = isinstance(im, int)
                if not static:
                    pe.wait_ge(s_var, (im - 2) * VAR + VAR)
                if not (static and im == 0):
                    sum_partitions(im - 1, 1 - par)
                for c in range(1, NCHUNK):
                    sum_chunk(im, par, c)
            sum_partitions(B - 1, 1)

            pe.wait_ge(s_const, 16)
            pe.wait_ge(s_wsplit, 24)
            pe.wait_ge(s_init, 6)

            def project(dst, col, par, width=128):
                n = 0
                for wt, xv in ((win_lo, xhi), (win_hi, xlo), (win_hi, xhi)):
                    for k in range(KC):
                        last = pe.matmul(dst, wt[:, k, col:col + width], xv[:, par, k], start=(n == 0), stop=(n == 3 * KC - 1))
                        n += 1
                return last

            def z_tile(r, m):
                if not r.exists():
                    return
                bank = wait_free(pe, r, "z", m)
                wait(pe, "xl", r, 3)
                project(bank[:, :], 128 * m, r.parity).then_inc(sem["z_mm"], 1)

            def y_transposed(q, m):
                if not q.exists():
                    return
                bank = wait_free(pe, q, "yT", m)
                wait(pe, "yn", q, 4)
                for p in range(PR):
                    last = pe.transpose(bank[:, 128 * p:128 * p + 128], y[:, p, 128 * m:128 * m + 128], ident)
                last.then_inc(sem["yT_mm"], 1)

            def x_transposed(n, k):
                if not n.exists():
                    return
                bank = wait_free(pe, n, "xT", k)
                wait(pe, "xn", n, 2)
                for p in range(PR):
                    last = pe.transpose(bank[:, 128 * p:128 * p + 128], xt[:, p, 128 * k:128 * k + 128], ident)
                last.then_inc(sem["xT_mm"], 1)

            def conv_input(t, tile):
                if not t.exists():
                    return
                o = 0 if tile == BC else tile + 1
                wait(pe, "tapb", t, 2 * (o - 1))
                wait(pe, "xl", t, 3)
                if o in (1, 2):
                    wait(pe, "dtv", t, o - 1)
                if tile == BC:
                    last = project(conv_bank(t, tile)[0:BCW, :], 2 * DI, t.parity, BCW)
                else:
                    last = project(conv_bank(t, tile)[:, :], DI + 128 * tile, t.parity)
                last.then_inc(sem["cv_mm"], 1)

            def out_pair(q, p):
                if not q.exists():
                    return
                bank = wait_free(pe, q, "out", p)
                wait(pe, "ylo", q, p + 1)
                if q.first() and p == 0:
                    pe.wait_ge(s_wosplit, 2)
                n = 0
                for yv, wt in ((yhi, wout_lo), (ylo, wout_hi), (yhi, wout_hi)):
                    for m in range(MT):
                        last = pe.matmul(bank[:, 0:C], yv[:, p % 2, m], wt[:, m, :], start=(n == 0), stop=(n == 3 * MT - 1))
                        n += 1
                last.then_inc(sem["out_mm"], 1)

            def decay_sums(r):
                if not r.exists():
                    return
                bank = wait_free(pe, r, "se", 0)
                wait(pe, "dch", r, 16)
                a = dA[:, r.parity].rearrange("p a h -> p (a h)")
                pe.matmul(bank[:, 0:48], cst[:, LATER:LATER + 128], a, start=True, stop=True)
                pe.matmul(bank[:, 48:96], cst[:, UPTO:UPTO + 128], a, start=True, stop=True)
                for h in range(4):
                    rhs = dA[:, r.parity].rearrange("p a (g h) -> p a g h", h=4)[:, :, :, h]
                    last = pe.matmul(bank[32 * h:32 * h + 32, 96:108].rearrange("p (a g) -> p a g", a=PR), sameimg, rhs,
                                     start=True, stop=True)
                last.then_inc(sem["se_mm"], 1)

            def b_and_c(r):
                if not r.exists():
                    return
                bank = wait_free(pe, r, "bcg", 0)
                wait(pe, "bc_act", r, 2)
                settle(pe)
                for p in range(PR):
                    for i in range(2):
                        tok = slice(128 * p + 64 * i, 128 * p + 64 * i + 64)
                        pe.matmul(bank[64 * i:64 * i + 64, 64 * p:64 * p + 64], bcB[:, tok], bcC[:, tok], start=True, stop=True)
                for m, v in enumerate((bcB, bcC)):
                    for p in range(PR):
                        at = 256 + 64 * m + 16 * p
                        last = pe.transpose(bank[:, at:at + NS], v[:, 128 * p:128 * p + 128], cst[0:NS, IDENT:IDENT + NS])
                last.then_inc(sem["bcg_mm"], 1)

            def x_tokens(r, j):
                if not r.exists():
                    return
                bank = wait_free(pe, r, "xk", j)
                wait(pe, "xc_act", r, j + 1)
                for p in range(PR):
                    last = pe.transpose(bank[:, 128 * p:128 * p + 128], xc[:, j % 2, 128 * p:128 * p + 128], ident)
                last.then_inc(sem["xk_mm"], 1)

            def decay_matrix(r, m):
                if not r.exists():
                    return
                bank = wait_free(pe, r, "df", m)
                wait(pe, "R", r, m + 1)
                for part in range(2):
                    last = pe.matmul(bank[:, :], later_r[:, :], R[:, part].rearrange("p h l -> p (h l)"),
                                     start=(part == 0), stop=(part == 1))
                last.then_inc(sem["df_mm"], 1)

            def c_channels(r, g):
                if not r.exists():
                    return
                bank = wait_free(pe, r, "cet", g)
                wait(pe, "ce", r, g + 1)
                for p in range(PR):
                    last = pe.transpose(bank[:, 128 * p:128 * p + 128], CE[:, p].rearrange("p h n -> p (h n)"), ident)
                last.then_inc(sem["cet_mm"], 1)

            def y_from_state(r, g):
                if not r.exists():
                    return
                wait(pe, "yv", r, 2 * g)
                wait(pe, "cet", r, g + 1)
                wait(pe, "sbd", r, g + 1)
                for p in range(PR):
                    for b in range(2):
                        rows = slice(64 * b, 64 * b + 64)
                        last = pe.matmul(ybank[b][:, 128 * p:128 * p + 128], CET[rows, p], Sbd[rows, p].rearrange("p h d -> p (h d)"),
                                         start=(p == 0), stop=False, skip_group_check=True)
                last.then_inc(sem["yo_mm"], 1)

            def y_in_row(r, g, half):
                if not r.exists():
                    return
                slot = (r.parity + g) % 2
                wait(pe, "Mv", r, 2 * g + 1 + half)
                wait(pe, "xd", r, g + 1)
                settle(pe)
                for p in (2 * half, 2 * half + 1):
                    for hh in range(2):
                        for i, b in ((0, 0), (1, 1), (0, 1), (1, 0)):
                            h = 2 * b + hh
                            rows = slice(64 * i, 64 * i + 64)
                            at = 128 * p + 64 * hh
                            last = pe.matmul(ybank[b][rows, at:at + 64], L[rows, p, h], Xd[rows, slot, p, 64 * h:64 * h + 64],
                                             start=False, stop=True, skip_group_check=True)
                last.then_inc(sem["y_mm"], 1)

            def scan_state(r, g):
                if not r.exists():
                    return
                slot = (r.parity + g) % 2
                bank = wait_free(pe, r, "st", g)
                wait(pe, "be", r, g + 1)
                wait(pe, "xd", r, g + 1)
                for p in range(PR):
                    for h in range(4):
                        last = pe.matmul(bank[32 * h:32 * h + 32, 64 * p:64 * p + 64], BE[:, p, h],
                                         Xd[:, slot, p, 64 * h:64 * h + 64], start=True, stop=True)
                last.then_inc(sem["st_mm"], 1)

            def dt_tokens(t):
                if not t.exists():
                    return
                bank = wait_free(pe, t, "dtT", 0)
                wait(pe, "dtv", t, 1)
                settle(pe)
                for p in range(PR):
                    last = pe.transpose(bank[:, NH * p:NH * p + NH], dtv[:, 128 * p:128 * p + 128], cst[0:NH, IDENT:IDENT + NH])
                last.then_inc(sem["dtT_mm"], 1)

            for n, t, r, q in steps(pe):
                for m in range(2, 4):
                    y_transposed(q, m)
                c_channels(r, 1)
                x_tokens(r, 1)
                y_from_state(r, 0)
                conv_input(t, 3)
                y_transposed(q, 4)
                scan_state(r, 0)
                y_in_row(r, 0, 0)
                y_transposed(q, 5)
                decay_matrix(r, 2)
                y_in_row(r, 0, 1)
                x_tokens(r, 2)
                z_tile(r, 0)
                conv_input(t, 4)
                y_from_state(r, 1)
                for m in range(0, 2):
                    out_pair(q, m)
                z_tile(r, 1)
                conv_input(t, 5)
                x_tokens(r, 3)
                decay_matrix(r, 3)
                for m in range(2, 6):
                    z_tile(r, m)
                for m in range(4, 6):
                    x_tokens(r, m)
                y_in_row(r, 1, 0)
                for m in range(0, 3):
                    x_transposed(n, m)
                y_in_row(r, 1, 1)
                decay_matrix(r, 4)
                c_channels(r, 2)
                conv_input(n, BC)
                scan_state(r, 1)
                decay_matrix(r, 5)
                dt_tokens(n)
                conv_input(n, 0)
                y_from_state(r, 2)
                out_pair(q, 2)
                y_in_row(r, 2, 0)
                y_in_row(r, 2, 1)
                decay_matrix(t, 0)
                out_pair(q, 3)
                decay_matrix(t, 1)
                b_and_c(t)
                decay_sums(t)
                conv_input(n, 1)
                c_channels(t, 0)
                x_tokens(t, 0)
                for m in range(0, 2):
                    y_transposed(r, m)
                conv_input(n, 2)
                scan_state(r, 2)


_INS = ["x", "L0_conv_W_in", "L0_conv_W_conv", "L0_conv_b_conv", "L0_conv_dt_bias", "L0_conv_A_log",
        "L0_conv_D_param", "L0_conv_gamma", "L0_conv_beta", "L0_conv_W_out"]


def kernel(**inputs):
    import numpy as _np
    import concourse.bacc as _bacc
    from concourse import mybir as _mybir
    from concourse.bass_utils import run_bass_kernel_spmd as _run

    nc = _bacc.Bacc("TRN2", target_bir_lowering=False, num_devices=1)
    arrays, args = {}, []
    tiles = lambda v: _np.ascontiguousarray(_np.asarray(v).reshape(MT, 128).T)
    laid = {name: _np.asarray(inputs[name]) for name in _INS[:2]}
    laid["W_conv"] = _np.asarray(inputs["L0_conv_W_conv"]).reshape(9, DI + 2 * NS).T
    laid["b_conv_x"] = tiles(inputs["L0_conv_b_conv"][:DI])
    laid["b_conv_bc"] = _np.asarray(inputs["L0_conv_b_conv"])[DI:, None]
    for name in _INS[4:7]:
        laid[name] = _np.asarray(inputs[name])
    laid["gamma"], laid["beta"] = tiles(inputs["L0_conv_gamma"]), tiles(inputs["L0_conv_beta"])
    laid["W_out"] = _np.asarray(inputs["L0_conv_W_out"])
    for name, a in laid.items():
        a = _np.ascontiguousarray(a)
        arrays[f"in_{name}_dram"] = a
        args.append(nc.dram_tensor(f"in_{name}_dram", a.shape, _mybir.dt.from_np(a.dtype), kind="ExternalInput").ap())
    c = constants()
    arrays["in_consts_dram"] = c
    args.append(nc.dram_tensor("in_consts_dram", c.shape, F32, kind="ExternalInput").ap())
    o = nc.dram_tensor("out_0_dram", (B, H, W, C), F32, kind="ExternalOutput").ap()
    build(nc, *args, o)
    r = _run(nc, [arrays], core_ids=[0])
    return r.results[0]["out_0_dram"]
```
